# Optimizing a Trainium2 kernel written in Bass

```python
import numpy as np
import jax
import jax.numpy as jnp

def _softmax(x, axis=-1):
    return jax.nn.softmax(x, axis=axis)

def _gelu(x):
    return jax.nn.gelu(x, approximate=True)

def _silu(x):
    return jax.nn.silu(x)

def _sigmoid(x):
    return jax.nn.sigmoid(x)

def _layernorm(x, axis=-1, eps=1e-05):
    m = jnp.mean(x, axis=axis, keepdims=True)
    v = jnp.var(x, axis=axis, keepdims=True)
    return (x - m) / jnp.sqrt(v + eps)

def _scatter_add(tgt, idx, src, axis=0):
    return tgt.at[idx].add(src)

def _segment_sum(src, seg, n):
    return jax.ops.segment_sum(src, seg, n)
kernel_name = 'mk_cond_resid_d2_seqx_r2_cde14d'

def setup_inputs(seed: int=0):
    np.random.seed(seed)
    _w = jnp.asarray

    def _rec_inputs():
        import jax
        import jax.numpy as jnp
        _rk = jax.random.key(seed)
        x = -0.0002928 + 1 * jax.random.normal(jax.random.fold_in(_rk, 1), (8, 1024, 512), jnp.float32)
        _lenS = 1024 - jax.random.randint(jax.random.fold_in(_rk, 7), (8,), 0, max(1, 1024 // 4) + 1, jnp.int32)
        _lenS2 = 1024 - jax.random.randint(jax.random.fold_in(_rk, 8), (8,), 0, max(1, 1024 // 4) + 1, jnp.int32)
        cond_1024 = -0.00356592 + 0.997978 * jax.random.normal(jax.random.fold_in(_rk, 11), (8, 512), jnp.float32)
        return (x, cond_1024)
    x, cond_1024 = _rec_inputs()

    def _L0_cond_setup():
        import jax, jax.numpy as jnp
        import numpy as np
        B, T, D = (128, 32, 512)
        ADA, INTER, RANK = (512, 512, 8)
        LN_EPS = 1e-05

        def _layernorm(x, g, b):
            mu = jnp.mean(x, axis=-1, keepdims=True)
            var = jnp.var(x, axis=-1, keepdims=True)
            return (x - mu) * jax.lax.rsqrt(var + LN_EPS) * g + b
        key = jax.random.key(seed)
        ks = jax.random.split(key, 9)
        return {'x': jax.random.normal(ks[0], (B, T, D), dtype=jnp.float32), 'ada_emb': jax.random.normal(ks[1], (B, ADA), dtype=jnp.float32), 'base_layer': jax.random.normal(ks[2], (D, D), dtype=jnp.float32), 'w1': jax.random.normal(ks[3], (ADA, INTER), dtype=jnp.float32) * 0.02, 'b1': jnp.zeros((INTER,), dtype=jnp.float32), 'w2': jax.random.normal(ks[4], (INTER, 2 * D * RANK), dtype=jnp.float32) * 0.02, 'b2': jnp.zeros((2 * D * RANK,), dtype=jnp.float32), 'ln_g': jnp.ones((ADA,), dtype=jnp.float32), 'ln_b': jnp.zeros((ADA,), dtype=jnp.float32)}
    _L0_cond_all = _L0_cond_setup()
    _L0_cond_in = {k: v for k, v in _L0_cond_all.items() if k in ('base_layer', 'w1', 'b1', 'w2', 'b2', 'ln_g', 'ln_b')}
    del _L0_cond_all

    def _L1_cond_setup():
        import jax, jax.numpy as jnp
        import numpy as np
        IN_FEATURES = 512
        OUT_FEATURES = 512
        BATCH = 32
        SEQ = 512
        EPS = 1e-08
        key = jax.random.key(seed)
        k1, k2, k3 = jax.random.split(key, 3)
        Efou = jax.random.normal(k1, (BATCH, SEQ, IN_FEATURES), dtype=jnp.float32)
        y = jax.random.normal(k2, (BATCH, IN_FEATURES), dtype=jnp.float32)
        weight = jax.random.normal(k3, (IN_FEATURES, OUT_FEATURES), dtype=jnp.float32)
        return {'Efou': Efou, 'y': y, 'weight': weight}
    _L1_cond_all = _L1_cond_setup()
    _L1_cond_in = {k: v for k, v in _L1_cond_all.items() if k in ('weight',)}
    del _L1_cond_all
    return {'x': x, 'cond_1024': cond_1024, 'L0_cond_base_layer': _L0_cond_in['base_layer'], 'L0_cond_w1': _L0_cond_in['w1'], 'L0_cond_b1': _L0_cond_in['b1'], 'L0_cond_w2': _L0_cond_in['w2'], 'L0_cond_b2': _L0_cond_in['b2'], 'L0_cond_ln_g': _L0_cond_in['ln_g'], 'L0_cond_ln_b': _L0_cond_in['ln_b'], 'L1_cond_weight': _L1_cond_in['weight']}

def reference(x, cond_1024, L0_cond_base_layer, L0_cond_w1, L0_cond_b1, L0_cond_w2, L0_cond_b2, L0_cond_ln_g, L0_cond_ln_b, L1_cond_weight):
    import jax
    import jax.numpy as jnp

    def _L0_cond_ref(x, ada_emb, base_layer, w1, b1, w2, b2, ln_g, ln_b):
        import jax, jax.numpy as jnp
        import numpy as np
        B, T, D = (128, 32, 512)
        ADA, INTER, RANK = (512, 512, 8)
        LN_EPS = 1e-05

        def _layernorm(x, g, b):
            mu = jnp.mean(x, axis=-1, keepdims=True)
            var = jnp.var(x, axis=-1, keepdims=True)
            return (x - mu) * jax.lax.rsqrt(var + LN_EPS) * g + b
        b, t, d = x.shape
        ae = _layernorm(ada_emb, ln_g, ln_b)
        h = jax.nn.gelu(ae @ w1 + b1, approximate=False)
        xw = h @ w2 + b2
        x_a, x_b = jnp.split(xw, 2, axis=-1)
        x_a = x_a.reshape(b, d, RANK)
        x_b = x_b.reshape(b, d, RANK)
        layer = base_layer[None, :, :] + jnp.einsum('bdr,bkr->bdk', x_a, x_b)
        out = jnp.einsum('btc,bco->bto', x, layer)
        return x + out

    def _L1_cond_ref(Efou, y, weight):
        import jax, jax.numpy as jnp
        import numpy as np
        IN_FEATURES = 512
        OUT_FEATURES = 512
        BATCH = 32
        SEQ = 512
        EPS = 1e-08
        scale = 1.0 / np.sqrt(np.float32(weight.shape[0]))
        ys = y * scale
        d = jax.lax.rsqrt(jnp.einsum('bi,io->bo', ys * ys, weight * weight) + EPS)
        out = jnp.einsum('bsi,io->bso', Efou * ys[:, None, :], weight) * d[:, None, :]
        return out
    x = x + _L0_cond_ref(x, cond_1024, L0_cond_base_layer, L0_cond_w1, L0_cond_b1, L0_cond_w2, L0_cond_b2, L0_cond_ln_g, L0_cond_ln_b)
    x = x + _L1_cond_ref(x, cond_1024, L1_cond_weight)
    return x

_drawn_inputs = setup_inputs


def setup_inputs(seed=0):
    import zlib

    import numpy as np

    out = dict(_drawn_inputs(seed))
    spreads = {'L0_cond_b1': (0.0, 0.465),
     'L0_cond_b2': (0.0, 0.1),
     'L0_cond_ln_g': (1.0, 0.6),
     'L0_cond_ln_b': (0.0, 0.8)}
    factors = {}
    for name, (base, spread) in spreads.items():
        noise = np.random.default_rng([zlib.crc32(name.encode()), seed]).standard_normal(out[name].shape)
        drawn = base * np.exp(spread * noise) if base else spread * noise
        out[name] = jnp.asarray(drawn.astype(out[name].dtype))
    for name, factor in factors.items():
        out[name] = (out[name] * factor).astype(out[name].dtype)
    return out
```

```python
from contextlib import ExitStack

import concourse.bass as bass
from concourse import mybir


ALU = mybir.AluOpType
ACT = mybir.ActivationFunctionType
F32 = mybir.dt.float32
F32R = mybir.dt.float32r

P = 128
B = 8
T = 1024
D = 512
RANK = 8
KC = D // P
HALVES = 2
TH = T // HALVES
TT = TH // P
UNITS = 16
LOOPED = 4
BANKS = 4
RTMP = 2
LN_EPS = 1e-5
D_EPS = 1e-8
YS_SCALE = float(D) ** -0.5


def cond_residual_kernel(nc, xT, condT, w0T, w1n, wm, b1c, lngc, lnbc, w2u, b2q, out):
    ctx = ExitStack()
    with ctx:
        def sb(name, shape, dt=F32):
            return ctx.enter_context(nc.sbuf_tensor(name, shape, dt))

        def sem(name):
            return ctx.enter_context(nc.semaphore(name))

        base = sb("base", [P, B, KC, D])
        w0s = sb("w0s", [P, 2, KC, D], F32R)
        pev = sb("pev", [P, 2, KC, D], F32R)
        rs = sb("rs", [P, KC, 2, D], F32R)
        w1s = sb("w1s", [P, KC, D])
        rtmp = sb("rtmp", [P, RTMP, D])
        stream = sb("stream", [P, 2, KC, D])
        xr = sb("xr", [P, 2, 2, TH])
        xs = sb("xs", [P, HALVES, 2, KC, TH], F32R)
        dsp = sb("dsp", [P, D], F32R)
        dmk = sb("dmk", [P, D], F32R)
        asp = sb("asp", [P, D], F32R)
        amk = sb("amk", [P, 2, D], F32R)
        chi = sb("chi", [P, D], F32R)
        clo = sb("clo", [P, D], F32R)
        ysb = sb("ysb", [P, KC, 64])
        ones = sb("ones", [P, P])
        onesr = sb("onesr", [P, P], F32R)
        ident = sb("ident", [P, P])
        sel2 = sb("sel2", [16, P])
        eye4 = sb("eye4", [P, 4, 4])
        sel3 = sb("sel3", [P, 16, B])
        mask = sb("mask", [P, B])
        cond = sb("cond", [P, KC, B])
        prm = sb("prm", [P, 3, KC])
        ys = sb("ys", [P, B, KC])
        lns = sb("lns", [P, 16, KC * B])
        w1sq, w0raw, wms = base[:, 3], base[:, 4], base[:, 5]
        hz = base[:, 6, 0, 0:KC * 32].rearrange("p (k r b) -> p k r b", k=KC, r=4)
        da, du, dv = base[:, 6, 1, :], base[:, 6, 2, :], base[:, 6, 3, :]
        ysq = du.rearrange("p (k q b) -> p k q b", k=KC, q=16)
        dfull, ab, ct = base[:, 7, 0, :], base[:, 7, 1, :], base[0:64, 7, 2, :]
        b2s = base[0:16, 7, 3, :]

        tiles = [ctx.enter_context(nc.psum_tensor(f"tile{i}", [P, D], F32)) for i in range(BANKS)]
        acc2 = ctx.enter_context(nc.psum_tensor("acc2", [P, D], F32))
        dbc = ctx.enter_context(nc.psum_tensor("dbc", [P, D], F32))
        aux = [ctx.enter_context(nc.psum_tensor(f"aux{i}", [P, D], F32)) for i in range(2)]

        small_loaded = sem("small_loaded")
        w1_loaded = sem("w1_loaded")
        w0_loaded = sem("w0_loaded")
        wm_loaded = sem("wm_loaded")
        b2_loaded = sem("b2_loaded")
        stream_dma = [sem(f"stream_dma{i}") for i in range(2)]
        x_loaded = [sem(f"x_loaded{i}") for i in range(2)]
        consts_ready = sem("consts_ready")
        pool_step = sem("pool_step")
        mask_ready = sem("mask_ready")
        ys_ready = sem("ys_ready")
        w1sq_ready = sem("w1sq_ready")
        ysq_ready = sem("ysq_ready")
        d2_done = sem("d2_done")
        sum_done = sem("sum_done")
        ln_step = sem("ln_step")
        ln_root = sem("ln_root")
        d_step = sem("d_step")
        d_root = sem("d_root")
        d_hi = sem("d_hi")
        dsp_ready = sem("dsp_ready")
        dmk_ready = sem("dmk_ready")
        dbc_ready = sem("dbc_ready")
        w0_eyed = sem("w0_eyed")
        w0_hi = sem("w0_hi")
        w0_lo = sem("w0_lo")
        h_done = sem("h_done")
        z_ready = sem("z_ready")
        h_ready = sem("h_ready")
        hz_ready = sem("hz_ready")
        acc2_steps = sem("acc2_steps")
        r_used = sem("r_used")
        r_scaled = sem("r_scaled")
        r_eyed = sem("r_eyed")
        r_hi = sem("r_hi")
        r_lo = sem("r_lo")
        tile_done = sem("tile_done")
        bank_free = sem("bank_free")
        ab_ready = sem("ab_ready")
        a_hi = sem("a_hi")
        a_lo = sem("a_lo")
        amk_ready = sem("amk_ready")
        bt_done = sem("bt_done")
        ysb_ready = sem("ysb_ready")
        c_done = sem("c_done")
        c_step = sem("c_step")
        c_hi = sem("c_hi")
        c_lo = sem("c_lo")
        ac_done = sem("ac_done")
        p_summed = sem("p_summed")
        p_hi = sem("p_hi")
        p_lo = sem("p_lo")
        x_hi = sem("x_hi")
        x_lo = sem("x_lo")

        def p_split(parity):
            return w0s if parity else pev

        block = ctx.enter_context(nc.Block())

        @block.sync
        def _(sp):
            def load_w2(unit, slot):
                sp.dma_start(stream[:, slot], w2u[unit]).then_inc(stream_dma[slot], 16)

            def load_x(b, h):
                for cp in range(2):
                    sp.dma_start(xr[:, cp], xT[b, h, cp]).then_inc(x_loaded[cp], 16)

            sp.dma_start(cond[:], condT).then_inc(small_loaded, 16)
            sp.dma_start(w1s[:, 0:2], w1n[:, 0:2]).then_inc(w1_loaded, 16)
            sp.dma_start(w1s[:, 2:4], w1n[:, 2:4]).then_inc(w1_loaded, 16)
            sp.dma_start(prm[:, 0], b1c).then_inc(small_loaded, 16)
            sp.dma_start(prm[:, 1], lngc).then_inc(small_loaded, 16)
            sp.dma_start(prm[:, 2], lnbc).then_inc(small_loaded, 16)
            sp.dma_start(w0raw, w0T).then_inc(w0_loaded, 16)
            sp.dma_start(wms, wm).then_inc(wm_loaded, 16)
            sp.dma_start(b2s, b2q).then_inc(b2_loaded, 16)
            load_w2(0, 0)
            load_w2(1, 1)
            with sp.Fori(0, LOOPED - 1) as b:
                for j in range(4):
                    sp.wait_ge(acc2_steps, b * 4 + (j + 2))
                    load_w2(b * 4 + (j + 2), j % 2)
            for j in range(2):
                sp.wait_ge(acc2_steps, UNITS - 2 + j)
                load_w2(UNITS - 2 + j, j)
            load_x(0, 0)
            for cp in range(2):
                sp.wait_ge(x_lo, cp + 1)
                sp.dma_start(xr[:, cp], xT[0, 1, cp]).then_inc(x_loaded[cp], 16)

            def store(b, h):
                sp.wait_ge(bank_free, b * 8 + (BANKS + 4 * B + 4 * h + 4))
                sp.dma_start(out[b, h], stream[:, h]).then_inc(stream_dma[h], 16)

            with sp.Fori(0, B - 1) as b:
                for h in range(HALVES):
                    for cp in range(2):
                        sp.wait_ge(x_lo, b * 4 + (4 + 2 * h + cp - 1))
                        sp.dma_start(xr[:, cp], xT[b + 1, h, cp]).then_inc(x_loaded[cp], 16)
                    store(b, h)
            for h in range(HALVES):
                store(B - 1, h)
            for h in range(HALVES):
                sp.wait_ge(stream_dma[h], 16 * (UNITS // 2 + B))

        @block.gpsimd
        def _(pool):
            nc.gpsimd.memset(ones[:], 1.0).then_inc(pool_step, 1)
            nc.gpsimd.memset(onesr[:].bitcast(F32), 1.0 / RANK).then_inc(pool_step, 1)
            nc.gpsimd.memset(sel3[:], 0.0).then_inc(pool_step, 1)
            nc.gpsimd.memset(eye4[:], 0.0).then_inc(pool_step, 1)
            pool.wait_ge(pool_step, 4)
            nc.gpsimd.affine_select(out=sel3[:], in_=sel3[:], compare_op=ALU.not_equal, fill=1.0, base=0,
                                    pattern=[[-8, 16], [-1, B]], channel_multiplier=1).then_inc(consts_ready, 1)
            nc.gpsimd.affine_select(out=ident[:], in_=ones[:], compare_op=ALU.is_equal, fill=0.0, base=0,
                                    pattern=[[-1, P]], channel_multiplier=1).then_inc(consts_ready, 1)
            nc.gpsimd.affine_select(out=eye4[:], in_=eye4[:], compare_op=ALU.not_equal, fill=1.0, base=0,
                                    pattern=[[-1, 4], [1, 4]], channel_multiplier=0).then_inc(consts_ready, 1)
            nc.gpsimd.affine_select(out=sel2[:], in_=ones[0:16, :], compare_op=ALU.is_ge, fill=0.0, base=0,
                                    pattern=[[1, P]], channel_multiplier=-8).then_inc(pool_step, 1)
            pool.wait_ge(pool_step, 5)
            nc.gpsimd.affine_select(out=sel2[:], in_=sel2[:], compare_op=ALU.is_ge, fill=0.0, base=7,
                                    pattern=[[-1, P]], channel_multiplier=8).then_inc(consts_ready, 1)
            pool.wait_ge(mask_ready, 1)
            pool.wait_ge(dsp_ready, 1)
            nc.gpsimd.tensor_tensor(dmk[:], dsp[:].bitcast(F32), mask[:, 0:1].to_broadcast([P, D]),
                                    ALU.mult).then_inc(dmk_ready, 1)
            with pool.Fori(1, B) as b:
                pool.wait_ge(dbc_ready, b)
                nc.gpsimd.tensor_tensor(dmk[:], dsp[:].bitcast(F32), mask[:, bass.ds(b, 1)].to_broadcast([P, D]),
                                        ALU.mult).then_inc(dmk_ready, 1)
            pool.wait_ge(a_lo, 1)
            for b in range(2):
                nc.gpsimd.tensor_scalar(amk[:, b], asp[:].bitcast(F32), mask[:, b:b + 1], None,
                                        ALU.mult).then_inc(amk_ready, 1)
            with pool.Fori(1, B // 2) as pair:
                for j in range(2):
                    pool.wait_ge(ac_done, pair * 8 + (4 * j - 4))
                    nc.gpsimd.tensor_tensor(amk[:, j], asp[:].bitcast(F32),
                                            mask[:, bass.ds(pair * 2 + j, 1)].to_broadcast([P, D]),
                                            ALU.mult).then_inc(amk_ready, 1)

        @block.scalar
        def _(act):
            act.wait_ge(w1_loaded, 32)
            for kc in range(KC):
                nc.scalar.activation(w1sq[:, kc], w1s[:, kc], ACT.Square).then_inc(w1sq_ready, 1)
            act.wait_ge(ln_step, 4)
            nc.scalar.activation(lns[:, 3, 0:B], lns[:, 2, 0:B], ACT.Sqrt).then_inc(ln_root, 1)
            act.wait_ge(w0_eyed, KC)
            nc.scalar.copy(w0s[:, 0], w0raw).then_inc(w0_hi, 1)
            act.wait_ge(d_step, 1)
            nc.scalar.activation(du, da, ACT.Sqrt).then_inc(d_root, 1)
            act.wait_ge(d_step, 5)
            nc.scalar.copy(dsp[:], dfull).then_inc(d_hi, 1)

            def r_high(b, kc):
                act.wait_ge(r_eyed, b * KC + (kc + 1))
                nc.scalar.copy(rs[:, kc, 0], rtmp[:, kc % RTMP]).then_inc(r_hi, 1)

            def evacuate_base(b):
                for cc in range(KC):
                    act.wait_ge(tile_done, b * KC + (cc + 1))
                    nc.scalar.copy(base[:, b, cc, :], tiles[cc][:]).then_inc(bank_free, 1)

            for kc in range(KC):
                r_high(0, kc)
            act.wait_ge(z_ready, 1)
            nc.scalar.activation(lns[:, 15], lns[:, 11], ACT.Gelu).then_inc(h_ready, 1)

            def base_step(b):
                for kc in range(KC - 1):
                    r_high(b + 1, kc)
                evacuate_base(b)
                r_high(b + 1, KC - 1)

            with act.Fori(0, LOOPED) as b:
                base_step(b)
            act.wait_ge(ab_ready, 1)
            nc.scalar.copy(asp[0:64, :], ab[64:128, :]).then_inc(a_hi, 1)
            nc.scalar.copy(asp[64:128, :], ab[64:128, :]).then_inc(a_hi, 1)
            base_step(4)
            base_step(5)
            act.wait_ge(c_step, 2)
            nc.scalar.copy(chi[0:64, :], ct).then_inc(c_hi, 1)
            nc.scalar.copy(chi[64:128, :], ct).then_inc(c_hi, 1)
            base_step(6)

            def x_high(b, h, cp, next_half=0):
                act.wait_ge(x_loaded[cp], b * 32 + 16 * (h + 1))
                if next_half:
                    act.wait_ge(tile_done, b * 8 + (4 * B + 4 * h - 4))
                nc.scalar.copy(xs[:, h, 0, 2 * cp:2 * cp + 2, :], xr[:, cp]).then_inc(x_hi, 1)

            def p_high(b, parity, cc):
                act.wait_ge(p_summed, b * KC + (cc + 1))
                nc.scalar.copy(p_split(parity)[:, 0, cc], base[:, b, cc, :]).then_inc(p_hi, 1)

            x_high(0, 0, 0)
            x_high(0, 0, 1)
            for cc in range(KC):
                p_high(0, 0, cc)
            act.wait_ge(c_lo, 2)
            evacuate_base(B - 1)

            def evacuate_out(b, h, tt):
                act.wait_ge(tile_done, b * 8 + (4 * B + 4 * h + tt + 1))
                if tt == 0:
                    act.wait_ge(stream_dma[h], b * 16 + 16 * (UNITS // 2))
                nc.scalar.copy(stream[:, h, tt, :], tiles[tt][:]).then_inc(bank_free, 1)

            def main_step(b, parity, last=False):
                for cp in range(2):
                    x_high(b, 1, cp, 1)
                    evacuate_out(b, 0, cp)
                for tt in (2, 3):
                    evacuate_out(b, 0, tt)
                for cp in range(2):
                    if not last:
                        x_high(b + 1, 0, cp, 1)
                        p_high(b + 1, 1 - parity, 2 * cp)
                        p_high(b + 1, 1 - parity, 2 * cp + 1)
                    evacuate_out(b, 1, cp)
                for tt in (2, 3):
                    evacuate_out(b, 1, tt)

            with act.Fori(0, B // 2 - 1) as pair:
                main_step(pair * 2, 0)
                main_step(pair * 2 + 1, 1)
            main_step(B - 2, 0)
            main_step(B - 1, 1, last=True)

        @block.vector
        def _(dve):
            small = [0]

            def step(instruction):
                small[0] += 1
                instruction.then_inc(ln_step, 1)
                dve.wait_ge(ln_step, small[0])

            def row(i, n=KC * B):
                return lns[:, i, 0:n]

            def by_chunk(i):
                return lns[:, i].rearrange("p (k b) -> p k b", k=KC)

            def over_chunks(i):
                return lns[:, i, 0:B].rearrange("p (k b) -> p k b", k=1).to_broadcast([P, KC, B])

            dve.wait_ge(small_loaded, 64)
            nc.vector.tensor_scalar(ys[:].rearrange("p b k -> p k b"), cond[:], YS_SCALE, None,
                                    ALU.mult).then_inc(ys_ready, 1)
            dve.wait_ge(ys_ready, 1)
            ys_wide = ys[:].rearrange("p b (k o) -> p k o b", o=1).to_broadcast([P, KC, 16, B])
            nc.vector.tensor_tensor(ysq, ys_wide, ys_wide, ALU.mult).then_inc(ysq_ready, 1)
            dve.wait_ge(sum_done, 1)
            step(nc.vector.tensor_scalar(row(0, B), aux[0][:, 0:B], 1.0 / D, None, ALU.mult))
            step(nc.vector.tensor_tensor(by_chunk(1), cond[:], over_chunks(0), ALU.subtract))
            step(nc.vector.tensor_tensor(row(4), row(1), row(1), ALU.mult))
            dve.wait_ge(sum_done, 2)
            step(nc.vector.tensor_scalar(row(2, B), aux[0][:, 64:64 + B], 1.0 / D, LN_EPS, ALU.mult, ALU.add))
            dve.wait_ge(ln_root, 1)
            step(nc.vector.reciprocal(row(5, B), row(3, B)))
            step(nc.vector.scalar_tensor_tensor(row(6, B), row(5, B), -0.5, row(2, B), ALU.mult, ALU.mult))
            step(nc.vector.tensor_tensor(row(7, B), row(6, B), row(5, B), ALU.mult))
            step(nc.vector.scalar_tensor_tensor(row(0, B), row(7, B), 1.5, row(5, B), ALU.add, ALU.mult))
            step(nc.vector.tensor_tensor(by_chunk(8), by_chunk(1), over_chunks(0), ALU.mult))
            step(nc.vector.tensor_tensor(by_chunk(9), by_chunk(8), prm[:, 1].to_broadcast([P, KC, B]), ALU.mult))
            step(nc.vector.tensor_tensor(by_chunk(10), by_chunk(9), prm[:, 2].to_broadcast([P, KC, B]), ALU.add))
            dve.wait_ge(consts_ready, 4)
            nc.vector.tensor_reduce(mask[:], sel3[:].rearrange("p q b -> p b q"), mybir.AxisListType.X,
                                    ALU.add).then_inc(mask_ready, 1)
            dve.wait_ge(w0_loaded, 16)
            for kc in range(KC):
                blk = w0raw[:, kc, kc * P:(kc + 1) * P]
                nc.vector.scalar_tensor_tensor(blk, ident[:], 2.0, blk, ALU.mult, ALU.add).then_inc(w0_eyed, 1)
            dve.wait_ge(d2_done, 1)
            nc.vector.tensor_scalar(da, aux[1][:], D_EPS, None, ALU.add).then_inc(d_step, 1)
            dve.wait_ge(w0_hi, 1)
            nc.vector.tensor_tensor(w0s[:, 1], w0raw, w0s[:, 0].bitcast(F32), ALU.subtract).then_inc(w0_lo, 1)
            dve.wait_ge(d_root, 1)
            nc.vector.reciprocal(dv, du).then_inc(d_step, 1)
            dve.wait_ge(d_step, 2)
            nc.vector.scalar_tensor_tensor(du, dv, -0.5, da, ALU.mult, ALU.mult).then_inc(d_step, 1)
            dve.wait_ge(d_step, 3)
            nc.vector.tensor_tensor(da, du, dv, ALU.mult).then_inc(d_step, 1)
            dve.wait_ge(d_step, 4)
            nc.vector.scalar_tensor_tensor(dfull, da, 1.5, dv, ALU.add, ALU.mult).then_inc(d_step, 1)
            dve.wait_ge(d_hi, 1)
            nc.vector.tensor_tensor(dsp[64:128, :], dfull[64:128, :], dsp[64:128, :].bitcast(F32),
                                    ALU.subtract).then_inc(dsp_ready, 1)

            def r_scale(b, kc, first):
                slot = rtmp[:, kc % RTMP]
                if not first and kc == KC - 1:
                    dve.wait_ge(tile_done, b * KC)
                elif not first:
                    dve.wait_ge(r_used, b * (KC - 1) + (kc + 1 - (KC - 1)))
                if not first or kc >= RTMP:
                    dve.wait_ge(r_lo, b * KC + (kc + 1 - RTMP))
                nc.vector.scalar_tensor_tensor(slot, w1s[:, kc], ys[:, bass.ds(b, 1), kc], dbc[:], ALU.mult,
                                               ALU.mult).then_inc(r_scaled, 1)
                dve.wait_ge(r_scaled, b * KC + (kc + 1))
                blk = slot[:, kc * P:(kc + 1) * P]
                nc.vector.tensor_tensor(blk, blk, ident[:], ALU.add).then_inc(r_eyed, 1)

            def r_low(b, kc):
                dve.wait_ge(r_hi, b * KC + (kc + 1))
                nc.vector.tensor_tensor(rs[:, kc, 1], rtmp[:, kc % RTMP], rs[:, kc, 0].bitcast(F32),
                                        ALU.subtract).then_inc(r_lo, 1)

            def r_build(b, first=False):
                dve.wait_ge(dbc_ready, b + 1)
                r_scale(b, 0, first)
                r_scale(b, 1, first)
                r_low(b, 0)
                r_low(b, 1)
                r_scale(b, 2, first)
                r_low(b, 2)
                r_scale(b, 3, first)
                r_low(b, 3)

            r_build(0, first=True)
            dve.wait_ge(h_done, 1)
            nc.vector.tensor_tensor(by_chunk(11), aux[0][:, 128:160].rearrange("p (k b) -> p k b", k=KC),
                                    prm[:, 0].to_broadcast([P, KC, B]), ALU.add).then_inc(z_ready, 1)
            dve.wait_ge(h_ready, 1)
            with dve.Fori(0, LOOPED) as b:
                dve.wait_ge(acc2_steps, b * 4 + 1)
                nc.vector.tensor_tensor(hz, lns[:, 15].rearrange("p (k o b) -> p k o b", k=KC, o=1)
                                        .to_broadcast([P, KC, 4, B]),
                                        eye4[:, bass.ds(b, 1), :].rearrange("p o (r c) -> p o r c", c=1)
                                        .to_broadcast([P, KC, 4, B]), ALU.mult).then_inc(hz_ready, 1)
                r_build(b + 1)
            dve.wait_ge(acc2_steps, UNITS + 1)
            nc.vector.tensor_copy(ab, acc2[:]).then_inc(ab_ready, 1)
            dve.wait_ge(a_hi, 2)
            nc.vector.tensor_tensor(asp[64:128, :], ab[64:128, :], asp[64:128, :].bitcast(F32),
                                    ALU.subtract).then_inc(a_lo, 1)
            r_build(5)
            dve.wait_ge(bt_done, 1)
            nc.vector.tensor_tensor(ysb[:].rearrange("p k (r b) -> p k r b", b=B),
                                    aux[0][:, 0:KC * 64].rearrange("p (k r b) -> p k r b", k=KC, b=B),
                                    ys[:].rearrange("p b (k o) -> p k o b", o=1).to_broadcast([P, KC, RANK, B]),
                                    ALU.mult).then_inc(ysb_ready, 1)
            r_build(6)
            dve.wait_ge(c_done, 1)
            nc.vector.tensor_tensor(ct, aux[1][0:64, :], dfull[0:64, :], ALU.mult).then_inc(c_step, 1)
            dve.wait_ge(c_step, 1)
            nc.vector.tensor_tensor(ct, ct, ab[0:64, :], ALU.add).then_inc(c_step, 1)
            dve.wait_ge(c_hi, 2)
            nc.vector.tensor_tensor(clo[0:64, :], ct, chi[0:64, :].bitcast(F32), ALU.subtract).then_inc(c_lo, 1)
            nc.vector.tensor_tensor(clo[64:128, :], ct, chi[0:64, :].bitcast(F32), ALU.subtract).then_inc(c_lo, 1)
            r_build(7)

            def x_low(b, h, cp):
                unit = b * 4 + (2 * h + cp + 1)
                dve.wait_ge(x_hi, unit)
                nc.vector.tensor_tensor(xs[:, h, 1, 2 * cp:2 * cp + 2, :], xr[:, cp],
                                        xs[:, h, 0, 2 * cp:2 * cp + 2, :].bitcast(F32),
                                        ALU.subtract).then_inc(x_lo, 1)

            def p_sum(b, cc):
                dve.wait_ge(ac_done, b * KC + (cc + 1))
                dve.wait_ge(bank_free, b * KC + (BANKS + cc + 1))
                nc.vector.tensor_tensor(base[:, b, cc, :], aux[cc % 2][:], base[:, b, cc, :],
                                        ALU.add).then_inc(p_summed, 1)

            def p_low(b, parity, cc):
                dve.wait_ge(p_hi, b * KC + (cc + 1))
                nc.vector.tensor_tensor(p_split(parity)[:, 1, cc], base[:, b, cc, :],
                                        p_split(parity)[:, 0, cc].bitcast(F32), ALU.subtract).then_inc(p_lo, 1)

            for cp in range(2):
                x_low(0, 0, cp)
            for cc in range(KC):
                p_sum(0, cc)
            for cc in range(KC):
                p_low(0, 0, cc)

            def main_step(b, parity, last=False):
                for cp in range(2):
                    x_low(b, 1, cp)
                if last:
                    return
                for cc in range(KC):
                    p_sum(b + 1, cc)
                for cp in range(2):
                    x_low(b + 1, 0, cp)
                    p_low(b + 1, 1 - parity, 2 * cp)
                    p_low(b + 1, 1 - parity, 2 * cp + 1)

            with dve.Fori(0, B // 2 - 1) as pair:
                main_step(pair * 2, 0)
                main_step(pair * 2 + 1, 1)
            main_step(B - 2, 0)
            main_step(B - 1, 1, last=True)

        @block.tensor
        def _(pe):
            pe.sem_inc(bank_free, BANKS)
            pe.wait_ge(small_loaded, 64)
            pe.wait_ge(pool_step, 4)
            for kc in range(KC):
                last = nc.tensor.matmul(aux[0][:, 0:B], ones[:], cond[:, kc], start=kc == 0, stop=kc == KC - 1)
            last.then_inc(sum_done, 1)
            pe.wait_ge(ln_step, 3)
            for kc in range(KC):
                last = nc.tensor.matmul(aux[0][:, 64:64 + B], ones[:], lns[:, 4, kc * B:(kc + 1) * B],
                                        start=kc == 0, stop=kc == KC - 1)
            last.then_inc(sum_done, 1)
            pe.wait_ge(ysq_ready, 1)
            for kc in range(KC):
                pe.wait_ge(w1sq_ready, kc + 1)
                last = nc.tensor.matmul(aux[1][:], ysq[:, kc], w1sq[:, kc], start=kc == 0, stop=kc == KC - 1)
            last.then_inc(d2_done, 1)
            pe.wait_ge(wm_loaded, 16)
            pe.wait_ge(ln_step, 11)
            for ic in range(KC):
                for kc in range(KC):
                    last = nc.tensor.matmul(aux[0][:, 128 + ic * B:128 + (ic + 1) * B],
                                            wms[:, kc, ic * P:(ic + 1) * P], lns[:, 10, kc * B:(kc + 1) * B],
                                            start=kc == 0, stop=kc == KC - 1)
            last.then_inc(h_done, 1)
            pe.wait_ge(b2_loaded, 16)
            pe.wait_ge(consts_ready, 4)
            nc.tensor.matmul(acc2[:], sel2[:], b2s, start=True, stop=True,
                             skip_group_check=True).then_inc(acc2_steps, 1)

            def spread_d(b):
                pe.wait_ge(dmk_ready, b + 1)
                nc.tensor.matmul(dbc[:], onesr[:], dmk[:], start=True, stop=True).then_inc(dbc_ready, 1)

            spread_d(0)
            pe.wait_ge(w0_lo, 1)

            def w2_unit(b, j):
                pe.wait_ge(hz_ready, b + 1)
                pe.wait_ge(stream_dma[j % 2], b * 32 + 16 * (j // 2 + 1))
                for g in range(4):
                    last = nc.tensor.matmul(acc2[32 * g:32 * g + 32, :], hz[:, j], stream[:, j % 2, g, :],
                                            start=False, stop=True, skip_group_check=True)
                last.then_inc(acc2_steps, 1)

            def base_tiles(b, units=False, spread=True):
                for kc in range(KC):
                    pe.wait_ge(r_lo, b * KC + (kc + 1))
                    for cc in range(KC):
                        if kc == 0:
                            pe.wait_ge(bank_free, b * KC + (cc + 1))
                        cols = slice(cc * P, (cc + 1) * P)
                        for i, (u, v) in enumerate(((0, 0), (1, 0), (0, 1))):
                            last = nc.tensor.matmul(tiles[cc][:], w0s[:, u, kc, cols], rs[:, kc, v],
                                                    start=kc == 0 and i == 0, stop=kc == KC - 1 and i == 2)
                        if kc == KC - 1:
                            last.then_inc(tile_done, 1)
                        elif cc == KC - 1:
                            last.then_inc(r_used, 1)
                    if units:
                        w2_unit(b, kc)
                    if spread and kc == 1:
                        pe.wait_ge(r_scaled, b * KC + KC)
                        spread_d(b + 1)

            def rank_tile(b, parity, cc, first=False):
                pe.wait_ge(amk_ready, b + 1)
                if not first or cc >= 2:
                    pe.wait_ge(p_summed, b * KC + (cc - 1))
                cols = slice(cc * P, (cc + 1) * P)
                nc.tensor.matmul(aux[cc % 2][:], amk[:, parity, cols], chi[:], start=True, stop=False)
                nc.tensor.matmul(aux[cc % 2][:], amk[:, parity, cols], clo[:], start=False,
                                 stop=True).then_inc(ac_done, 1)

            with pe.Fori(0, LOOPED) as b:
                base_tiles(b, units=True)
            base_tiles(4)
            pe.wait_ge(ab_ready, 1)
            for kc in range(KC):
                last = nc.tensor.transpose(aux[0][:, kc * 64:(kc + 1) * 64], ab[0:64, kc * P:(kc + 1) * P],
                                           ident[0:64, 0:64])
            last.then_inc(bt_done, 1)
            base_tiles(5)
            pe.wait_ge(ysb_ready, 1)
            for kc in range(KC):
                last = nc.tensor.matmul(aux[1][0:64, :], ysb[:, kc], w1s[:, kc], start=kc == 0, stop=kc == KC - 1)
            last.then_inc(c_done, 1)
            base_tiles(6)
            pe.wait_ge(c_lo, 2)
            for cc in range(KC):
                rank_tile(0, 0, cc, first=True)
            base_tiles(7, spread=False)

            def main_step(b, parity, last=False):
                pe.wait_ge(p_lo, b * KC + KC)
                for h in range(HALVES):
                    pe.wait_ge(x_lo, b * 4 + (2 * h + 2))
                    for tt in range(TT):
                        pe.wait_ge(bank_free, b * 8 + (4 * B + 4 * h + tt + 1))
                        toks = slice(tt * P, (tt + 1) * P)
                        n = 0
                        for cc in range(KC):
                            for u, v in ((0, 0), (1, 0), (0, 1)):
                                mm = nc.tensor.matmul(tiles[tt][:], xs[:, h, u, cc, toks],
                                                      p_split(parity)[:, v, cc], start=n == 0, stop=n == 11)
                                n += 1
                        mm.then_inc(tile_done, 1)
                        if h == 0 and not last:
                            rank_tile(b + 1, 1 - parity, tt)

            with pe.Fori(0, B // 2 - 1) as pair:
                main_step(pair * 2, 0)
                main_step(pair * 2 + 1, 1)
            main_step(B - 2, 0)
            main_step(B - 1, 1, last=True)


def kernel(**inputs):
    import numpy as np
    import concourse.bacc as bacc
    from concourse.bass_utils import run_bass_kernel_spmd

    def chunked(a):
        return np.ascontiguousarray(a.reshape(KC, P, -1).transpose(1, 0, 2))

    def columns(a):
        return np.ascontiguousarray(a.reshape(KC, P).T)

    a = {k: np.asarray(v) for k, v in inputs.items()}
    x = a["x"].reshape(B, HALVES, P, TT, 2, 2, P)
    x = np.ascontiguousarray(x.transpose(0, 1, 4, 6, 5, 3, 2)).reshape(B, HALVES, 2, P, 2, TH)
    w2 = a["L0_cond_w2"].reshape(KC, P, 2, D, 2, 4)[:, :, ::-1]
    w2 = np.ascontiguousarray(w2.transpose(5, 0, 1, 2, 4, 3)).reshape(UNITS, P, 4, D)
    b2 = np.ascontiguousarray(a["L0_cond_b2"].reshape(2, D, RANK)[::-1].transpose(0, 2, 1)).reshape(16, D)
    arrays = {
        "xT": x,
        "condT": chunked(a["cond_1024"].T),
        "w0T": chunked(a["L0_cond_base_layer"].T),
        "w1n": chunked(a["L1_cond_weight"]),
        "wm": chunked(a["L0_cond_w1"]),
        "b1c": columns(a["L0_cond_b1"]),
        "lngc": columns(a["L0_cond_ln_g"]),
        "lnbc": columns(a["L0_cond_ln_b"]),
        "w2u": w2,
        "b2q": b2,
    }
    nc = bacc.Bacc("TRN2", target_bir_lowering=False, num_devices=1)
    aps = {k: nc.dram_tensor(f"in_{k}", v.shape, F32, kind="ExternalInput").ap() for k, v in arrays.items()}
    out = nc.dram_tensor("out", (B, HALVES, P, TT, D), F32, kind="ExternalOutput").ap()
    cond_residual_kernel(nc, out=out, **aps)
    r = run_bass_kernel_spmd(nc, [{f"in_{k}": v for k, v in arrays.items()}], core_ids=[0])
    return r.results[0]["out"].reshape(B, T, D)
```

```python
from contextlib import ExitStack

import concourse.bass as bass
from concourse import mybir


ALU = mybir.AluOpType
ACT = mybir.ActivationFunctionType
F32 = mybir.dt.float32
F32R = mybir.dt.float32r

P = 128
B = 8
T = 1024
D = 512
RANK = 8
KC = D // P
HALVES = 2
TH = T // HALVES
TT = TH // P
UNITS = 16
LOOPED = 4
BANKS = 4
WARM_UP = 8
RTMP = 2
LN_EPS = 1e-5
D_EPS = 1e-8
YS_SCALE = float(D) ** -0.5


def cond_residual_kernel(nc, xT, condT, w0T, w1n, wm, b1c, lngc, lnbc, w2u, b2q, out):
    ctx = ExitStack()
    with ctx:
        def sb(name, shape, dt=F32):
            return ctx.enter_context(nc.sbuf_tensor(name, shape, dt))

        def sem(name):
            return ctx.enter_context(nc.semaphore(name))

        base = sb("base", [P, B, KC, D])
        w0s = sb("w0s", [P, 2, KC, D], F32R)
        pev = sb("pev", [P, 2, KC, D], F32R)
        rs = sb("rs", [P, KC, 2, D], F32R)
        w1s = sb("w1s", [P, KC, D])
        rtmp = sb("rtmp", [P, RTMP, D])
        stream = sb("stream", [P, 2, KC, D])
        xr = sb("xr", [P, 2, 2, TH])
        xs = sb("xs", [P, HALVES, 2, KC, TH], F32R)
        dgn = sb("dgn", [P, 2, KC, P], F32R)
        asq = sb("asq", [P, 2, D], F32R)
        csq = sb("csq", [P, 2, D], F32R)
        amk = sb("amk", [P, 2, D], F32R)
        ysb = sb("ysb", [P, KC, 64])
        ones = sb("ones", [P, P])
        onesr = sb("onesr", [P, P], F32R)
        ident = sb("ident", [P, P])
        sel2 = sb("sel2", [16, P])
        eye4 = sb("eye4", [P, 4, 4])
        sel3 = sb("sel3", [P, 32, 4])
        mask = sb("mask", [P, 2, 4])
        cond = sb("cond", [P, KC, B])
        prm = sb("prm", [P, 3, KC])
        ys = sb("ys", [P, B, KC])
        dts = sb("dts", [P, 2, B, KC])
        dth = sb("dth", [P, B, KC], F32R)
        lns = sb("lns", [P, 16, KC * B])
        w1sq, w0raw, wms = base[:, 3], base[:, 4], base[:, 5]
        hz = base[:, 6, 0, 0:KC * 32].rearrange("p (k r b) -> p k r b", k=KC, r=4)
        dt64 = base[:, 6, 1, 0:KC * 64].rearrange("p (k c) -> p k c", k=KC)
        d64, ab, ct = base[0:64, 7, 0, :], base[:, 7, 1, :], base[0:64, 7, 2, :]
        asp, csp = pev[:, 0, 0], pev[:, 0, 1]
        perm = pev[:, 0, 2].rearrange("p (o m) -> p o m", o=4)
        b2s = base[0:16, 7, 3, :]

        eye_wide = ident[:].rearrange("p (o m) -> p o m", o=1).to_broadcast([P, KC, P])

        tiles = [ctx.enter_context(nc.psum_tensor(f"tile{i}", [P, D], F32)) for i in range(BANKS)]
        acc2 = ctx.enter_context(nc.psum_tensor("acc2", [P, D], F32))
        dbc = ctx.enter_context(nc.psum_tensor("dbc", [P, D], F32))
        aux = [ctx.enter_context(nc.psum_tensor(f"aux{i}", [P, D], F32)) for i in range(2)]

        cond_loaded = sem("cond_loaded")
        prm_loaded = sem("prm_loaded")
        w1_loaded = [sem(f"w1_loaded{i}") for i in range(2)]
        w0_loaded = sem("w0_loaded")
        wm_loaded = sem("wm_loaded")
        b2_loaded = sem("b2_loaded")
        stream_dma = [sem(f"stream_dma{i}") for i in range(2)]
        x_loaded = [sem(f"x_loaded{i}") for i in range(2)]
        consts_ready = sem("consts_ready")
        pool_step = sem("pool_step")
        mask_ready = sem("mask_ready")
        ys_ready = sem("ys_ready")
        w1sq_ready = sem("w1sq_ready")
        ysq_ready = sem("ysq_ready")
        d2_done = sem("d2_done")
        sum_done = sem("sum_done")
        ln_step = sem("ln_step")
        ln_root = sem("ln_root")
        d_step = sem("d_step")
        d_root = sem("d_root")
        dgn_ready = sem("dgn_ready")
        d64_done = sem("d64_done")
        dt64_ready = sem("dt64_ready")
        d64_ready = sem("d64_ready")
        root_loaded = sem("root_loaded")
        perm_ready = sem("perm_ready")
        perm_done = sem("perm_done")
        squared = sem("squared")
        dbc_ready = sem("dbc_ready")
        w0_eyed = sem("w0_eyed")
        w0_hi = sem("w0_hi")
        w0_lo = sem("w0_lo")
        h_done = sem("h_done")
        z_ready = sem("z_ready")
        h_ready = sem("h_ready")
        hz_ready = sem("hz_ready")
        acc2_steps = sem("acc2_steps")
        r_used = sem("r_used")
        r_scaled = sem("r_scaled")
        r_eyed = sem("r_eyed")
        r_hi = sem("r_hi")
        r_lo = sem("r_lo")
        tile_done = sem("tile_done")
        bank_free = sem("bank_free")
        ab_ready = sem("ab_ready")
        a_hi = sem("a_hi")
        a_lo = sem("a_lo")
        amk_ready = sem("amk_ready")
        bt_done = sem("bt_done")
        ysb_ready = sem("ysb_ready")
        c_done = sem("c_done")
        c_step = sem("c_step")
        c_hi = sem("c_hi")
        c_lo = sem("c_lo")
        ac_done = sem("ac_done")
        p_summed = sem("p_summed")
        p_hi = sem("p_hi")
        p_lo = sem("p_lo")
        x_hi = sem("x_hi")
        x_lo = sem("x_lo")

        def p_split(parity):
            return w0s if parity else pev

        block = ctx.enter_context(nc.Block())

        @block.sync
        def _(sp):
            def load_w2(unit, slot):
                sp.dma_start(stream[:, slot], w2u[unit]).then_inc(stream_dma[slot], 16)

            def load_x(b, h):
                for cp in range(2):
                    sp.dma_start(xr[:, cp], xT[b, h, cp]).then_inc(x_loaded[cp], 16)

            sp.dma_start(cond[:], condT).then_inc(cond_loaded, 16)
            for i in range(2):
                sp.dma_start(w1s[:, 2 * i:2 * i + 2], w1n[:, 2 * i:2 * i + 2]).then_inc(w1_loaded[i], 16)
            sp.dma_start(w0raw, w0T).then_inc(w0_loaded, 16)
            for i, column in enumerate((b1c, lngc, lnbc)):
                sp.dma_start(prm[:, i], column).then_inc(prm_loaded, 16)
            sp.dma_start(wms, wm).then_inc(wm_loaded, 16)
            sp.dma_start(b2s, b2q).then_inc(b2_loaded, 16)
            load_w2(0, 0)
            load_w2(1, 1)
            with sp.Fori(0, LOOPED - 1) as b:
                for j in range(4):
                    sp.wait_ge(acc2_steps, b * 4 + (j + 2))
                    load_w2(b * 4 + (j + 2), j % 2)
            for j in range(2):
                sp.wait_ge(acc2_steps, UNITS - 2 + j)
                load_w2(UNITS - 2 + j, j)
            load_x(0, 0)
            for cp in range(2):
                sp.wait_ge(x_lo, cp + 1)
                sp.dma_start(xr[:, cp], xT[0, 1, cp]).then_inc(x_loaded[cp], 16)

            def store(b, h):
                sp.wait_ge(bank_free, b * 8 + (BANKS + 4 * B + 4 * h + 4))
                sp.dma_start(out[b, h], stream[:, h]).then_inc(stream_dma[h], 16)

            with sp.Fori(0, B - 1) as b:
                for h in range(HALVES):
                    for cp in range(2):
                        sp.wait_ge(x_lo, b * 4 + (4 + 2 * h + cp - 1))
                        sp.dma_start(xr[:, cp], xT[b + 1, h, cp]).then_inc(x_loaded[cp], 16)
                    store(b, h)
            store(B - 1, 0)
            for tt in range(TT):
                sp.wait_ge(bank_free, BANKS + 4 * B + 8 * (B - 1) + 4 + tt + 1)
                sp.dma_start(out[B - 1, 1, :, tt], stream[:, 1, tt]).then_inc(stream_dma[1], 16)
            sp.wait_ge(stream_dma[0], 16 * (UNITS // 2 + B))
            sp.wait_ge(stream_dma[1], 16 * (UNITS // 2 + B - 1 + TT))

        @block.gpsimd
        def _(pool):
            nc.gpsimd.memset(ones[:], 1.0).then_inc(pool_step, 1)
            nc.gpsimd.memset(onesr[:].bitcast(F32), 1.0).then_inc(pool_step, 1)
            nc.gpsimd.memset(sel3[:], 0.0).then_inc(pool_step, 1)
            nc.gpsimd.memset(eye4[:], 0.0).then_inc(pool_step, 1)
            pool.wait_ge(pool_step, 4)
            nc.gpsimd.affine_select(out=ident[:], in_=ones[:], compare_op=ALU.is_equal, fill=0.0, base=0,
                                    pattern=[[-1, P]], channel_multiplier=1).then_inc(consts_ready, 1)
            nc.gpsimd.affine_select(out=sel3[:], in_=sel3[:], compare_op=ALU.not_equal, fill=1.0, base=0,
                                    pattern=[[-4, 32], [-1, 4]], channel_multiplier=1).then_inc(consts_ready, 1)
            nc.gpsimd.affine_select(out=eye4[:], in_=eye4[:], compare_op=ALU.not_equal, fill=1.0, base=0,
                                    pattern=[[-1, 4], [1, 4]], channel_multiplier=0).then_inc(consts_ready, 1)
            nc.gpsimd.affine_select(out=sel2[:], in_=ones[0:16, :], compare_op=ALU.is_ge, fill=0.0, base=0,
                                    pattern=[[1, P]], channel_multiplier=-8).then_inc(pool_step, 1)
            pool.wait_ge(pool_step, 5)
            nc.gpsimd.affine_select(out=sel2[:], in_=sel2[:], compare_op=ALU.is_ge, fill=0.0, base=7,
                                    pattern=[[-1, P]], channel_multiplier=8).then_inc(consts_ready, 1)
            pool.wait_ge(consts_ready, 4)

            def spread_diagonals(b, parts=(0, 1)):
                for u in parts:
                    col = dts[:, u, bass.ds(b, 1), :].rearrange("p o (k m) -> p (o k) m", m=1)
                    nc.gpsimd.tensor_tensor(dgn[:, u], eye_wide, col.to_broadcast([P, KC, P]),
                                            ALU.mult).then_inc(dgn_ready, 1)

            pool.wait_ge(d_step, 5)
            spread_diagonals(0, parts=(0,))
            for kc in (2, 3):
                pool.wait_ge(w0_hi, kc + 1)
                nc.gpsimd.tensor_tensor(w0s[:, 1, kc], w0raw[:, kc], w0s[:, 0, kc].bitcast(F32),
                                        ALU.subtract).then_inc(w0_lo, 1)
            for c in range(2):
                for g in range(2):
                    for q in range(2):
                        src = ident[:, q * 64:(q + 1) * 64].rearrange("p (r b) -> p r b", b=B)[:, :, 4 * g:4 * g + 4]
                        dst = perm[:, 2 * c + g].rearrange("p (u v r b) -> p u v r b", u=2, v=2, b=4)
                        for i in range(2):
                            at = dst[:, q, i] if c else dst[:, i, q]
                            nc.gpsimd.tensor_copy(at, src).then_inc(perm_ready, 1)
            with pool.Fori(1, B) as b:
                pool.wait_ge(dbc_ready, b)
                spread_diagonals(b)
            pool.wait_ge(squared, 2)
            for b in range(2):
                nc.gpsimd.tensor_scalar(amk[:, b], asq[:, 0].bitcast(F32), mask[:, 0, b:b + 1], None,
                                        ALU.mult).then_inc(amk_ready, 1)
            with pool.Fori(1, B // 2) as pair:
                for j in range(2):
                    pool.wait_ge(ac_done, pair * 8 + (4 * j - 4))
                    keep = mask[:].rearrange("p g b -> p (g b)")[:, bass.ds(pair * 2 + j, 1)]
                    nc.gpsimd.tensor_tensor(amk[:, j], asq[:, bass.ds(pair // 2, 1), :].rearrange("p o n -> p (o n)")
                                            .bitcast(F32), keep.to_broadcast([P, D]),
                                            ALU.mult).then_inc(amk_ready, 1)

        @block.scalar
        def _(act):
            act.wait_ge(pool_step, 4)
            nc.scalar.activation(lns[:, 14, 0:1], ones[:, 0:1], ACT.Sqrt).then_inc(root_loaded, 1)
            for kc in range(KC):
                act.wait_ge(w1_loaded[kc // 2], 16)
                nc.scalar.activation(w1sq[:, kc], w1s[:, kc], ACT.Square).then_inc(w1sq_ready, 1)
            act.wait_ge(ln_step, 4)
            nc.scalar.activation(lns[:, 12, 0:B], lns[:, 2, 0:B], ACT.Sqrt).then_inc(ln_root, 1)

            def w0_high(kc):
                act.wait_ge(w0_eyed, kc + 1)
                nc.scalar.copy(w0s[:, 0, kc], w0raw[:, kc]).then_inc(w0_hi, 1)

            for kc in range(2):
                w0_high(kc)
            act.wait_ge(d_step, 1)
            nc.scalar.activation(lns[:, 4], lns[:, 3], ACT.Sqrt).then_inc(d_root, 1)
            for kc in (2, 3):
                w0_high(kc)

            def r_high(b, kc):
                act.wait_ge(r_eyed, b * KC + (kc + 1))
                nc.scalar.copy(rs[:, kc, 0], rtmp[:, kc % RTMP]).then_inc(r_hi, 1)

            def evacuate_base(b):
                for cc in range(KC):
                    act.wait_ge(tile_done, b * KC + (cc + 1))
                    nc.scalar.copy(base[:, b, cc, :], tiles[cc][:]).then_inc(bank_free, 1)

            for kc in range(3):
                r_high(0, kc)
            act.wait_ge(z_ready, 1)
            nc.scalar.activation(lns[:, 15], lns[:, 11], ACT.Gelu).then_inc(h_ready, 1)
            r_high(0, 3)

            def base_step(b):
                for kc in range(KC - 1):
                    r_high(b + 1, kc)
                evacuate_base(b)
                r_high(b + 1, KC - 1)

            with act.Fori(0, LOOPED) as b:
                base_step(b)
            act.wait_ge(ab_ready, 1)
            act.wait_ge(perm_ready, 16)
            nc.scalar.copy(asp[0:64, :], ab[64:128, :]).then_inc(a_hi, 1)
            nc.scalar.copy(asp[64:128, :], ab[64:128, :]).then_inc(a_hi, 1)

            def x_high(b, h, cp, next_half=0):
                act.wait_ge(x_loaded[cp], b * 32 + 16 * (h + 1))
                if next_half:
                    act.wait_ge(tile_done, b * 8 + (4 * B + 4 * h - 4))
                nc.scalar.copy(xs[:, h, 0, 2 * cp:2 * cp + 2, :], xr[:, cp]).then_inc(x_hi, 1)

            def squared_rows(to, g, bank, n):
                act.wait_ge(perm_done, n)
                nc.scalar.copy(to[:, g], bank[:]).then_inc(squared, 1)

            base_step(4)
            act.wait_ge(d64_done, 1)
            nc.scalar.copy(d64, aux[1][0:64, :]).then_inc(d64_ready, 1)
            x_high(0, 0, 0)
            x_high(0, 0, 1)
            base_step(5)
            squared_rows(asq, 0, acc2, 1)
            squared_rows(asq, 1, aux[0], 2)
            act.wait_ge(c_step, 2)
            nc.scalar.copy(csp[0:64, :], ct).then_inc(c_hi, 1)
            nc.scalar.copy(csp[64:128, :], ct).then_inc(c_hi, 1)

            def p_high(b, parity, cc):
                act.wait_ge(p_summed, b * KC + (cc + 1))
                nc.scalar.copy(p_split(parity)[:, 0, cc], base[:, b, cc, :]).then_inc(p_hi, 1)

            r_high(7, 0)
            r_high(7, 1)
            squared_rows(csq, 0, acc2, 3)
            squared_rows(csq, 1, aux[0], 4)
            r_high(7, 2)
            evacuate_base(6)
            r_high(7, KC - 1)
            for cc in range(KC):
                p_high(0, 0, cc)
            evacuate_base(B - 1)

            def evacuate_out(b, h, tt):
                act.wait_ge(tile_done, b * 8 + (4 * B + 4 * h + tt + 1))
                if tt == 0:
                    act.wait_ge(stream_dma[h], b * 16 + 16 * (UNITS // 2))
                nc.scalar.copy(stream[:, h, tt, :], tiles[tt][:]).then_inc(bank_free, 1)

            def main_step(b, parity, last=False):
                for cp in range(2):
                    x_high(b, 1, cp, 1)
                    evacuate_out(b, 0, cp)
                for tt in (2, 3):
                    evacuate_out(b, 0, tt)
                for cp in range(2):
                    if not last:
                        x_high(b + 1, 0, cp, 1)
                        p_high(b + 1, 1 - parity, 2 * cp)
                        p_high(b + 1, 1 - parity, 2 * cp + 1)
                    evacuate_out(b, 1, cp)
                for tt in (2, 3):
                    evacuate_out(b, 1, tt)

            with act.Fori(0, B // 2 - 1) as pair:
                main_step(pair * 2, 0)
                main_step(pair * 2 + 1, 1)
            main_step(B - 2, 0)
            main_step(B - 1, 1, last=True)

        @block.vector
        def _(dve):
            small = [0]

            def step(instruction):
                small[0] += 1
                instruction.then_inc(ln_step, 1)
                dve.wait_ge(ln_step, small[0])

            def row(i, n=KC * B):
                return lns[:, i, 0:n]

            def by_chunk(i):
                return lns[:, i].rearrange("p (k b) -> p k b", k=KC)

            def over_chunks(i):
                return lns[:, i, 0:B].rearrange("p (k b) -> p k b", k=1).to_broadcast([P, KC, B])

            dve.wait_ge(cond_loaded, 16)
            nc.vector.tensor_scalar(ys[:].rearrange("p b k -> p k b"), cond[:], YS_SCALE, None,
                                    ALU.mult).then_inc(ys_ready, 1)
            dve.wait_ge(ys_ready, 1)
            nc.vector.tensor_tensor(by_chunk(13), ys[:].rearrange("p b k -> p k b"),
                                    ys[:].rearrange("p b k -> p k b"), ALU.mult).then_inc(ysq_ready, 1)
            dve.wait_ge(sum_done, 1)
            step(nc.vector.tensor_scalar(row(0, B), aux[0][:, 0:B], 1.0 / D, None, ALU.mult))
            step(nc.vector.tensor_tensor(by_chunk(1), cond[:], over_chunks(0), ALU.subtract))
            step(nc.vector.tensor_tensor(row(5), row(1), row(1), ALU.mult))
            dve.wait_ge(consts_ready, 4)
            nc.vector.tensor_reduce(mask[:, 0], sel3[:].rearrange("p q b -> p b q"), mybir.AxisListType.X,
                                    ALU.add).then_inc(mask_ready, 1)
            dve.wait_ge(mask_ready, 1)
            nc.vector.tensor_copy(mask[:, 1], mask[:, 0]).then_inc(mask_ready, 1)

            def add_two(kc):
                blk = w0raw[:, kc, kc * P:(kc + 1) * P]
                nc.vector.scalar_tensor_tensor(blk, ident[:], 2.0, blk, ALU.mult, ALU.add).then_inc(w0_eyed, 1)

            dve.wait_ge(sum_done, 2)
            step(nc.vector.tensor_scalar(row(2, B), aux[0][:, 64:64 + B], 1.0 / D, LN_EPS, ALU.mult, ALU.add))
            dve.wait_ge(ln_root, 1)
            step(nc.vector.reciprocal(row(5, B), row(12, B)))
            step(nc.vector.scalar_tensor_tensor(row(6, B), row(5, B), -0.5, row(2, B), ALU.mult, ALU.mult))
            step(nc.vector.tensor_tensor(row(7, B), row(6, B), row(5, B), ALU.mult))
            step(nc.vector.scalar_tensor_tensor(row(0, B), row(7, B), 1.5, row(5, B), ALU.add, ALU.mult))
            dve.wait_ge(prm_loaded, 48)
            step(nc.vector.tensor_tensor(by_chunk(8), by_chunk(1), over_chunks(0), ALU.mult))
            step(nc.vector.tensor_tensor(by_chunk(9), by_chunk(8), prm[:, 1].to_broadcast([P, KC, B]), ALU.mult))
            step(nc.vector.tensor_tensor(by_chunk(10), by_chunk(9), prm[:, 2].to_broadcast([P, KC, B]), ALU.add))
            dve.wait_ge(w0_loaded, 16)
            for kc in range(KC):
                add_two(kc)
            dve.wait_ge(d2_done, 1)
            nc.vector.tensor_scalar(row(3), aux[1][:, 0:KC * B], D_EPS, None, ALU.add).then_inc(d_step, 1)
            dve.wait_ge(d_root, 1)
            nc.vector.reciprocal(row(6), row(4)).then_inc(d_step, 1)
            dve.wait_ge(d_step, 2)
            nc.vector.scalar_tensor_tensor(row(7), row(6), -0.5, row(3), ALU.mult, ALU.mult).then_inc(d_step, 1)
            dve.wait_ge(d_step, 3)
            nc.vector.tensor_tensor(row(8), row(7), row(6), ALU.mult).then_inc(d_step, 1)
            dve.wait_ge(d_step, 4)
            nc.vector.scalar_tensor_tensor(dts[:, 0].rearrange("p b k -> p k b"), by_chunk(8), 1.5, by_chunk(6),
                                           ALU.add, ALU.mult).then_inc(d_step, 1)
            dve.wait_ge(d_step, 5)
            nc.vector.tensor_copy(dth[:], dts[:, 0]).then_inc(d_root, 1)
            dve.wait_ge(d_root, 2)
            nc.vector.tensor_tensor(dts[:, 1], dts[:, 0], dth[:].bitcast(F32), ALU.subtract).then_inc(d_step, 1)
            dve.wait_ge(d_step, 6)
            low = dts[:, 1, 0].rearrange("p (k m) -> p k m", m=1).to_broadcast([P, KC, P])
            nc.vector.tensor_tensor(dgn[:, 1], eye_wide, low, ALU.mult).then_inc(dgn_ready, 1)
            for kc in range(2):
                dve.wait_ge(w0_hi, kc + 1)
                nc.vector.tensor_tensor(w0s[:, 1, kc], w0raw[:, kc], w0s[:, 0, kc].bitcast(F32),
                                        ALU.subtract).then_inc(w0_lo, 1)
            def r_scale(b, kc, first):
                slot = rtmp[:, kc % RTMP]
                if not first and kc == KC - 1:
                    dve.wait_ge(tile_done, b * KC)
                elif not first:
                    dve.wait_ge(r_used, b * (KC - 1) + (kc + 1 - (KC - 1)))
                if not first or kc >= RTMP:
                    dve.wait_ge(r_lo, b * KC + (kc + 1 - RTMP))
                nc.vector.scalar_tensor_tensor(slot, w1s[:, kc], ys[:, bass.ds(b, 1), kc], dbc[:], ALU.mult,
                                               ALU.mult).then_inc(r_scaled, 1)
                dve.wait_ge(r_scaled, b * KC + (kc + 1))
                blk = slot[:, kc * P:(kc + 1) * P]
                nc.vector.tensor_tensor(blk, blk, ident[:], ALU.add).then_inc(r_eyed, 1)

            def r_low(b, kc):
                dve.wait_ge(r_hi, b * KC + (kc + 1))
                nc.vector.tensor_tensor(rs[:, kc, 1], rtmp[:, kc % RTMP], rs[:, kc, 0].bitcast(F32),
                                        ALU.subtract).then_inc(r_lo, 1)

            def x_low(b, h, cp):
                unit = b * 4 + (2 * h + cp + 1)
                dve.wait_ge(x_hi, unit)
                nc.vector.tensor_tensor(xs[:, h, 1, 2 * cp:2 * cp + 2, :], xr[:, cp],
                                        xs[:, h, 0, 2 * cp:2 * cp + 2, :].bitcast(F32),
                                        ALU.subtract).then_inc(x_lo, 1)

            def h_columns(b):
                dve.wait_ge(acc2_steps, b * 4 + 1)
                nc.vector.tensor_tensor(hz, lns[:, 15].rearrange("p (k o b) -> p k o b", k=KC, o=1)
                                        .to_broadcast([P, KC, 4, B]),
                                        eye4[:, bass.ds(b, 1), :].rearrange("p o (r c) -> p o r c", c=1)
                                        .to_broadcast([P, KC, 4, B]), ALU.mult).then_inc(hz_ready, 1)

            def r_build(b, columns=False):
                dve.wait_ge(dbc_ready, b + 1)
                r_scale(b, 0, False)
                r_scale(b, 1, False)
                r_low(b, 0)
                r_low(b, 1)
                r_scale(b, 2, False)
                r_low(b, 2)
                r_scale(b, 3, False)
                if columns:
                    h_columns(b)
                r_low(b, 3)

            dve.wait_ge(dbc_ready, 1)
            r_scale(0, 0, True)
            r_scale(0, 1, True)
            r_low(0, 0)
            r_low(0, 1)
            dve.wait_ge(h_done, 1)
            nc.vector.tensor_tensor(by_chunk(11), aux[0][:, 128:160].rearrange("p (k b) -> p k b", k=KC),
                                    prm[:, 0].to_broadcast([P, KC, B]), ALU.add).then_inc(z_ready, 1)
            r_scale(0, 2, True)
            r_low(0, 2)
            dve.wait_ge(h_ready, 1)
            h_columns(0)
            r_scale(0, 3, True)
            r_low(0, 3)
            with dve.Fori(0, LOOPED - 1) as b:
                r_build(b + 1, columns=True)
            r_build(LOOPED)
            nc.vector.tensor_copy(dt64.rearrange("p k (r b) -> p k r b", b=B),
                                  dts[:, 0].rearrange("p b (k o) -> p k o b", o=1)
                                  .to_broadcast([P, KC, RANK, B])).then_inc(dt64_ready, 1)
            dve.wait_ge(acc2_steps, UNITS + 1)
            nc.vector.tensor_copy(ab, acc2[:]).then_inc(ab_ready, 1)
            dve.wait_ge(a_hi, 2)
            nc.vector.tensor_tensor(asp[64:128, :], ab[64:128, :], asp[64:128, :].bitcast(F32),
                                    ALU.subtract).then_inc(a_lo, 1)
            r_build(5)
            dve.wait_ge(bt_done, 1)
            nc.vector.tensor_tensor(ysb[:].rearrange("p k (r b) -> p k r b", b=B),
                                    aux[0][:, 0:KC * 64].rearrange("p (k r b) -> p k r b", k=KC, b=B),
                                    ys[:].rearrange("p b (k o) -> p k o b", o=1).to_broadcast([P, KC, RANK, B]),
                                    ALU.mult).then_inc(ysb_ready, 1)
            for cp in range(2):
                x_low(0, 0, cp)
            r_build(6)
            dve.wait_ge(c_done, 1)
            dve.wait_ge(d64_ready, 1)
            nc.vector.tensor_tensor(ct, aux[1][0:64, :], d64, ALU.mult).then_inc(c_step, 1)
            dve.wait_ge(c_step, 1)
            nc.vector.tensor_tensor(ct, ct, ab[0:64, :], ALU.add).then_inc(c_step, 1)
            dve.wait_ge(c_hi, 2)
            nc.vector.tensor_tensor(csp[64:128, :], ct, csp[0:64, :].bitcast(F32), ALU.subtract).then_inc(c_lo, 1)
            r_build(7)

            def p_sum(b, cc):
                dve.wait_ge(ac_done, b * KC + (cc + 1))
                dve.wait_ge(bank_free, b * KC + (BANKS + cc + 1))
                nc.vector.tensor_tensor(base[:, b, cc, :], aux[cc % 2][:], base[:, b, cc, :],
                                        ALU.add).then_inc(p_summed, 1)

            def p_low(b, parity, cc):
                dve.wait_ge(p_hi, b * KC + (cc + 1))
                nc.vector.tensor_tensor(p_split(parity)[:, 1, cc], base[:, b, cc, :],
                                        p_split(parity)[:, 0, cc].bitcast(F32), ALU.subtract).then_inc(p_lo, 1)

            for cc in range(KC):
                p_sum(0, cc)
            for cc in range(KC):
                p_low(0, 0, cc)

            def main_step(b, parity, last=False):
                for cp in range(2):
                    x_low(b, 1, cp)
                if last:
                    return
                for cc in range(KC):
                    p_sum(b + 1, cc)
                for cp in range(2):
                    x_low(b + 1, 0, cp)
                    p_low(b + 1, 1 - parity, 2 * cp)
                    p_low(b + 1, 1 - parity, 2 * cp + 1)

            with dve.Fori(0, B // 2 - 1) as pair:
                main_step(pair * 2, 0)
                main_step(pair * 2 + 1, 1)
            main_step(B - 2, 0)
            main_step(B - 1, 1, last=True)

        @block.tensor
        def _(pe):
            pe.sem_inc(bank_free, BANKS)
            pe.wait_ge(pool_step, 4)
            for _ in range(WARM_UP):
                nc.tensor.matmul(dbc[:, 0:P], ones[:], ones[:], start=True, stop=True)
            pe.wait_ge(cond_loaded, 16)
            for kc in range(KC):
                last = nc.tensor.matmul(aux[0][:, 0:B], ones[:], cond[:, kc], start=kc == 0, stop=kc == KC - 1)
            last.then_inc(sum_done, 1)
            pe.wait_ge(ln_step, 3)
            for kc in range(KC):
                last = nc.tensor.matmul(aux[0][:, 64:64 + B], ones[:], lns[:, 5, kc * B:(kc + 1) * B],
                                        start=kc == 0, stop=kc == KC - 1)
            last.then_inc(sum_done, 1)
            pe.wait_ge(ysq_ready, 1)
            for kc in range(KC):
                pe.wait_ge(w1sq_ready, kc + 1)
                for oc in range(KC):
                    last = nc.tensor.matmul(aux[1][:, oc * B:(oc + 1) * B], w1sq[:, kc, oc * P:(oc + 1) * P],
                                            lns[:, 13, kc * B:(kc + 1) * B], start=kc == 0 and oc == 0,
                                            stop=kc == KC - 1, skip_group_check=True)
            last.then_inc(d2_done, 1)
            def spread_d(b, first=False):
                pe.wait_ge(dgn_ready, b * 2 + (1 if not first else 2))
                nc.tensor.matmul(dbc[:], onesr[:], dgn[:, 0].rearrange("p k m -> p (k m)"), start=True, stop=False)
                pe.wait_ge(dgn_ready, b * 2 + 2)
                nc.tensor.matmul(dbc[:], onesr[:], dgn[:, 1].rearrange("p k m -> p (k m)"), start=False,
                                 stop=True).then_inc(dbc_ready, 1)

            pe.wait_ge(wm_loaded, 16)
            pe.wait_ge(ln_step, 11)
            for ic in range(KC):
                for kc in range(KC):
                    last = nc.tensor.matmul(aux[0][:, 128 + ic * B:128 + (ic + 1) * B],
                                            wms[:, kc, ic * P:(ic + 1) * P], lns[:, 10, kc * B:(kc + 1) * B],
                                            start=kc == 0, stop=kc == KC - 1)
            last.then_inc(h_done, 1)
            pe.wait_ge(b2_loaded, 16)
            pe.wait_ge(consts_ready, 4)
            nc.tensor.matmul(acc2[:], sel2[:], b2s, start=True, stop=True,
                             skip_group_check=True).then_inc(acc2_steps, 1)

            spread_d(0, first=True)
            pe.wait_ge(w0_lo, 4)

            def w2_unit(b, j):
                pe.wait_ge(hz_ready, b + 1)
                pe.wait_ge(stream_dma[j % 2], b * 32 + 16 * (j // 2 + 1))
                for g in range(4):
                    last = nc.tensor.matmul(acc2[32 * g:32 * g + 32, :], hz[:, j], stream[:, j % 2, g, :],
                                            start=False, stop=True, skip_group_check=True)
                last.then_inc(acc2_steps, 1)

            def base_tiles(b, units=False, spread=True, between=None):
                for kc in range(KC):
                    pe.wait_ge(r_lo, b * KC + (kc + 1))
                    for cc in range(KC):
                        if kc == 0:
                            pe.wait_ge(bank_free, b * KC + (cc + 1))
                        cols = slice(cc * P, (cc + 1) * P)
                        for i, (u, v) in enumerate(((0, 0), (0, 1), (1, 0))):
                            last = nc.tensor.matmul(tiles[cc][:], w0s[:, u, kc, cols], rs[:, kc, v],
                                                    start=kc == 0 and i == 0, stop=kc == KC - 1 and i == 2)
                        if kc == KC - 1:
                            last.then_inc(tile_done, 1)
                        elif cc == KC - 1:
                            last.then_inc(r_used, 1)
                    if units:
                        w2_unit(b, kc)
                    if between:
                        between(b, kc)
                    if spread and kc == 0:
                        pe.wait_ge(r_scaled, b * KC + KC)
                        spread_d(b + 1)

            def rank_tile(b, parity, cc, group, first=False):
                pe.wait_ge(amk_ready, b + 1)
                if not first or cc >= 2:
                    pe.wait_ge(p_summed, b * KC + (cc - 1))
                rows = csq[:, bass.ds(group, 1), :].rearrange("p o n -> p (o n)")
                nc.tensor.matmul(aux[cc % 2][:], amk[:, parity, cc * P:(cc + 1) * P], rows, start=True,
                                 stop=True).then_inc(ac_done, 1)

            def permute(bank, which, rows):
                nc.tensor.matmul(bank[:], perm[:, which], rows, start=True, stop=True).then_inc(perm_done, 1)

            with pe.Fori(0, LOOPED) as b:
                base_tiles(b, units=True)
            base_tiles(4)
            pe.wait_ge(ab_ready, 1)
            for kc in range(KC):
                last = nc.tensor.transpose(aux[0][:, kc * 64:(kc + 1) * 64], ab[0:64, kc * P:(kc + 1) * P],
                                           ident[0:64, 0:64])
            last.then_inc(bt_done, 1)
            pe.wait_ge(dt64_ready, 1)
            for kc in range(KC):
                last = nc.tensor.matmul(aux[1][0:64, kc * P:(kc + 1) * P], dt64[:, kc], ident[:], start=True,
                                        stop=True)
            last.then_inc(d64_done, 1)
            base_tiles(5)
            pe.wait_ge(ysb_ready, 1)
            pe.wait_ge(d64_ready, 1)
            for kc in range(KC):
                last = nc.tensor.matmul(aux[1][0:64, :], ysb[:, kc], w1s[:, kc], start=kc == 0, stop=kc == KC - 1)
            last.then_inc(c_done, 1)
            pe.wait_ge(a_lo, 1)
            permute(acc2, 0, asp)
            permute(aux[0], 1, asp)

            def permute_c(b, kc):
                if kc != 2:
                    return
                pe.wait_ge(c_lo, 1)
                pe.wait_ge(squared, 2)
                permute(acc2, 2, csp)
                permute(aux[0], 3, csp)

            base_tiles(6, between=permute_c)
            pe.wait_ge(squared, 4)
            for cc in range(2):
                rank_tile(0, 0, cc, 0, first=True)

            def rest_of_rank(b, kc):
                if kc < 2:
                    rank_tile(0, 0, kc + 2, 0, first=True)

            base_tiles(7, spread=False, between=rest_of_rank)

            def main_step(b, parity, group, last=False):
                pe.wait_ge(p_lo, b * KC + KC)
                for h in range(HALVES):
                    pe.wait_ge(x_lo, b * 4 + (2 * h + 2))
                    for tt in range(TT):
                        pe.wait_ge(bank_free, b * 8 + (4 * B + 4 * h + tt + 1))
                        toks = slice(tt * P, (tt + 1) * P)
                        n = 0
                        for cc in range(KC):
                            for u, v in ((0, 0), (0, 1), (1, 0)):
                                mm = nc.tensor.matmul(tiles[tt][:], xs[:, h, u, cc, toks],
                                                      p_split(parity)[:, v, cc], start=n == 0, stop=n == 11)
                                n += 1
                        mm.then_inc(tile_done, 1)
                        if h == 0 and not last:
                            rank_tile(b + 1, 1 - parity, tt, group)

            with pe.Fori(0, B // 2 - 1) as pair:
                main_step(pair * 2, 0, pair // 2)
                main_step(pair * 2 + 1, 1, (pair + 1) // 2)
            main_step(B - 2, 0, 1)
            main_step(B - 1, 1, None, last=True)


def kernel(**inputs):
    import numpy as np
    import concourse.bacc as bacc
    from concourse.bass_utils import run_bass_kernel_spmd

    def chunked(a):
        return np.ascontiguousarray(a.reshape(KC, P, -1).transpose(1, 0, 2))

    def columns(a):
        return np.ascontiguousarray(a.reshape(KC, P).T)

    a = {k: np.asarray(v) for k, v in inputs.items()}
    x = a["x"].reshape(B, HALVES, P, TT, 2, 2, P)
    x = np.ascontiguousarray(x.transpose(0, 1, 4, 6, 5, 3, 2)).reshape(B, HALVES, 2, P, 2, TH)
    w2 = a["L0_cond_w2"].reshape(KC, P, 2, D, 2, 4)[:, :, ::-1]
    w2 = np.ascontiguousarray(w2.transpose(5, 0, 1, 2, 4, 3)).reshape(UNITS, P, 4, D)
    b2 = np.ascontiguousarray(a["L0_cond_b2"].reshape(2, D, RANK)[::-1].transpose(0, 2, 1)).reshape(16, D)
    arrays = {
        "xT": x,
        "condT": chunked(a["cond_1024"].T),
        "w0T": chunked(a["L0_cond_base_layer"].T),
        "w1n": chunked(a["L1_cond_weight"]),
        "wm": chunked(a["L0_cond_w1"]),
        "b1c": columns(a["L0_cond_b1"]),
        "lngc": columns(a["L0_cond_ln_g"]),
        "lnbc": columns(a["L0_cond_ln_b"]),
        "w2u": w2,
        "b2q": b2,
    }
    nc = bacc.Bacc("TRN2", target_bir_lowering=False, num_devices=1)
    aps = {k: nc.dram_tensor(f"in_{k}", v.shape, F32, kind="ExternalInput").ap() for k, v in arrays.items()}
    out = nc.dram_tensor("out", (B, HALVES, P, TT, D), F32, kind="ExternalOutput").ap()
    cond_residual_kernel(nc, out=out, **aps)
    r = run_bass_kernel_spmd(nc, [{f"in_{k}": v for k, v in arrays.items()}], core_ids=[0])
    return r.results[0]["out"].reshape(B, T, D)
```

```python
from contextlib import ExitStack

import concourse.bass as bass
from concourse import mybir


ALU = mybir.AluOpType
ACT = mybir.ActivationFunctionType
F32 = mybir.dt.float32
F32R = mybir.dt.float32r

P = 128
B = 8
T = 1024
D = 512
RANK = 8
KC = D // P
HALVES = 2
TH = T // HALVES
TT = TH // P
UNITS = 16
LOOPED = 4
BANKS = 4
WARM_UP = (6, 3, 2)
RTMP = 2
LN_EPS = 1e-5
D_EPS = 1e-8
YS_SCALE = float(D) ** -0.5


def cond_residual_kernel(nc, xT, condT, w0T, w0n, w1n, wm, b1c, lngc, lnbc, w2u, b2q, out):
    ctx = ExitStack()
    with ctx:
        def sb(name, shape, dt=F32):
            return ctx.enter_context(nc.sbuf_tensor(name, shape, dt))

        def sem(name):
            return ctx.enter_context(nc.semaphore(name))

        base = sb("base", [P, B, KC, D])
        w0s = sb("w0s", [P, 2, KC, D], F32R)
        pev = sb("pev", [P, 2, KC, D], F32R)
        rs = sb("rs", [P, KC, 2, D], F32R)
        w1s = sb("w1s", [P, KC, D])
        rtmp = sb("rtmp", [P, RTMP, D])
        stream = sb("stream", [P, 2, KC, D])
        xr = sb("xr", [P, 2, 2, TH])
        xs = sb("xs", [P, HALVES, 2, KC, TH], F32R)
        dbs = sb("dbs", [P, D])
        asq = sb("asq", [P, 2, D], F32R)
        csq = sb("csq", [P, 2, D], F32R)
        amk = sb("amk", [P, 2, D], F32R)
        ysb = sb("ysb", [P, KC, 64])
        ones = sb("ones", [P, P])
        onesr = sb("onesr", [P, P], F32R)
        ident = sb("ident", [P, P])
        two_eye = sb("two_eye", [P, P])
        sel2 = sb("sel2", [16, P])
        eye4 = sb("eye4", [P, 4, 4])
        sel3 = sb("sel3", [P, 32, 4])
        mask = sb("mask", [P, 2, 4])
        cond = sb("cond", [P, KC, B])
        prm = sb("prm", [P, 3, KC])
        ys = sb("ys", [P, B, KC])
        dts = sb("dts", [P, 2, B, KC])
        dth = sb("dth", [P, B, KC], F32R)
        lns = sb("lns", [P, 16, KC * B])
        w1sq, w0raw, wms = base[:, 3], base[:, 4], base[:, 5]
        hz = base[:, 6, 0, 0:KC * 32].rearrange("p (k r b) -> p k r b", k=KC, r=4)
        ysq, ae = [base[:, 6, 2, i * P:(i + 1) * P].rearrange("p (k c) -> p k c", k=KC) for i in range(2)]
        d2_rows, h_rows = base[:, 6, 3, 0:P], base[:, 6, 3, P:2 * P]
        d64, ab, ct = base[0:64, 7, 0, :], base[:, 7, 1, :], base[0:64, 7, 2, :]
        d_rows = base[0:B * KC, 6, 3, 2 * P:3 * P]
        m0s, w1r = xs[:, 0], xs[:, 1]
        asp, csp = pev[:, 0, 0], pev[:, 0, 1]
        perm = pev[:, 0, 2].rearrange("p (o m) -> p o m", o=4)
        w0nat, d_first = stream[:, 1], stream[:, 0, 0]
        dgn = rs[:, KC - 1].rearrange("p u (k m) -> p u k m", k=KC)
        b2s, c_part = base[0:16, 7, 3, :], base[0:64, 7, 3, :]

        eye_wide = ident[:].rearrange("p (o m) -> p o m", o=1).to_broadcast([P, KC, P])

        d_kept = nc.dram_tensor("d_kept", (B, D), F32, kind="Internal").ap()

        tiles = [ctx.enter_context(nc.psum_tensor(f"tile{i}", [P, D], F32)) for i in range(BANKS)]
        acc2 = ctx.enter_context(nc.psum_tensor("acc2", [P, D], F32))
        dbc = ctx.enter_context(nc.psum_tensor("dbc", [P, D], F32))
        aux = [ctx.enter_context(nc.psum_tensor(f"aux{i}", [P, D], F32)) for i in range(2)]

        cond_loaded = sem("cond_loaded")
        prm_loaded = sem("prm_loaded")
        w1_loaded = [sem(f"w1_loaded{i}") for i in range(KC)]
        w0_loaded = [sem(f"w0_loaded{i}") for i in range(KC)]
        w0nat_loaded = sem("w0nat_loaded")
        wm_loaded = sem("wm_loaded")
        b2_loaded = sem("b2_loaded")
        stream_dma = [sem(f"stream_dma{i}") for i in range(2)]
        x_loaded = [sem(f"x_loaded{i}") for i in range(2)]
        consts_ready = sem("consts_ready")
        pool_step = sem("pool_step")
        mask_ready = sem("mask_ready")
        ys_ready = sem("ys_ready")
        w1sq_ready = sem("w1sq_ready")
        ysq_ready = sem("ysq_ready")
        d2_done = sem("d2_done")
        d2_copied = sem("d2_copied")
        d2_turned = sem("d2_turned")
        sum_done = sem("sum_done")
        ln_step = sem("ln_step")
        ln_root = sem("ln_root")
        d_step = sem("d_step")
        d_root = sem("d_root")
        dgn_ready = sem("dgn_ready")
        d_turned = sem("d_turned")
        d_copied = sem("d_copied")
        d_written = sem("d_written")
        dbs_loaded = sem("dbs_loaded")
        d64_loaded = sem("d64_loaded")
        d_first_loaded = sem("d_first_loaded")
        perm_ready = sem("perm_ready")
        perm_done = sem("perm_done")
        squared = sem("squared")
        dbc_ready = sem("dbc_ready")
        w0_eyed = sem("w0_eyed")
        w0_hi = sem("w0_hi")
        w0_lo = sem("w0_lo")
        m0_hi = sem("m0_hi")
        m0_lo = sem("m0_lo")
        w1_hi = sem("w1_hi")
        w1_lo = sem("w1_lo")
        fix_step = sem("fix_step")
        fixed = sem("fixed")
        ae_ready = sem("ae_ready")
        h_done = sem("h_done")
        h_copied = sem("h_copied")
        h_turned = sem("h_turned")
        z_ready = sem("z_ready")
        h_ready = sem("h_ready")
        hz_ready = sem("hz_ready")
        acc2_steps = sem("acc2_steps")
        r_used = sem("r_used")
        r_scaled = sem("r_scaled")
        r_eyed = sem("r_eyed")
        r_hi = sem("r_hi")
        r_lo = sem("r_lo")
        tile_done = sem("tile_done")
        bank_free = sem("bank_free")
        ab_ready = sem("ab_ready")
        a_hi = sem("a_hi")
        a_lo = sem("a_lo")
        amk_ready = sem("amk_ready")
        bt_done = sem("bt_done")
        ysb_ready = sem("ysb_ready")
        c_done = sem("c_done")
        c_halved = sem("c_halved")
        c_step = sem("c_step")
        c_hi = sem("c_hi")
        c_lo = sem("c_lo")
        ac_done = sem("ac_done")
        p_summed = sem("p_summed")
        p_hi = sem("p_hi")
        p_lo = sem("p_lo")
        x_hi = sem("x_hi")
        x_lo = sem("x_lo")

        def p_split(parity):
            return w0s if parity else pev

        block = ctx.enter_context(nc.Block())

        @block.sync
        def _(sp):
            def load_w2(unit, slot):
                sp.dma_start(stream[:, slot], w2u[unit]).then_inc(stream_dma[slot], 16)

            def load_x(b, h):
                for cp in range(2):
                    sp.dma_start(xr[:, cp], xT[b, h, cp]).then_inc(x_loaded[cp], 16)

            sp.dma_start(cond[:], condT).then_inc(cond_loaded, 16)
            for kc in range(KC):
                sp.dma_start(w0raw[:, kc], w0T[:, kc]).then_inc(w0_loaded[kc], 16)
                sp.dma_start(w1s[:, kc], w1n[:, kc]).then_inc(w1_loaded[kc], 16)
            for i, column in enumerate((b1c, lngc, lnbc)):
                sp.dma_start(prm[:, i], column).then_inc(prm_loaded, 16)
            sp.dma_start(b2s, b2q).then_inc(b2_loaded, 16)
            sp.dma_start(wms, wm).then_inc(wm_loaded, 16)
            load_w2(0, 0)
            load_w2(1, 1)

            def on_partitions(to, b):
                return sp.dma_start(to, d_kept[bass.ds(b, 1), :].to_broadcast([P, D]))

            def load_d(b):
                sp.wait_ge(r_scaled, b * KC - KC)
                on_partitions(dbs[:], b).then_inc(dbs_loaded, 16)

            sp.wait_ge(d_copied, 1)
            sp.dma_start(d_kept.rearrange("b (k m) -> (b k) m", k=KC), d_rows).then_inc(d_written, 16)
            sp.wait_ge(d_written, 16)
            for r in range(RANK):
                sp.dma_start(d64[r * B:(r + 1) * B, :], d_kept).then_inc(d64_loaded, 16)
            with sp.Fori(0, LOOPED - 1) as b:
                load_d(b + 2)
                for j in range(4):
                    sp.wait_ge(acc2_steps, b * 4 + (j + 2))
                    load_w2(b * 4 + (j + 2), j % 2)
            load_d(LOOPED + 1)
            for j in range(2):
                sp.wait_ge(acc2_steps, UNITS - 2 + j)
                load_w2(UNITS - 2 + j, j)
            load_x(0, 0)
            sp.wait_ge(acc2_steps, UNITS + 1)
            load_d(LOOPED + 2)
            sp.dma_start(w0nat, w0n).then_inc(w0nat_loaded, 16)
            on_partitions(d_first, 0).then_inc(d_first_loaded, 16)
            load_d(B - 1)
            for cp in range(2):
                sp.wait_ge(x_lo, cp + 1)
                sp.dma_start(xr[:, cp], xT[0, 1, cp]).then_inc(x_loaded[cp], 16)

            def store(b, h):
                sp.wait_ge(bank_free, b * 8 + (BANKS + 4 * B + 4 * h + 4))
                sp.dma_start(out[b, h], stream[:, h]).then_inc(stream_dma[h], 16)

            with sp.Fori(0, B - 1) as b:
                for h in range(HALVES):
                    for cp in range(2):
                        sp.wait_ge(x_lo, b * 4 + (4 + 2 * h + cp - 1))
                        sp.dma_start(xr[:, cp], xT[b + 1, h, cp]).then_inc(x_loaded[cp], 16)
                    store(b, h)
            store(B - 1, 0)
            for tt in range(TT):
                sp.wait_ge(bank_free, BANKS + 4 * B + 8 * (B - 1) + 4 + tt + 1)
                sp.dma_start(out[B - 1, 1, :, tt], stream[:, 1, tt]).then_inc(stream_dma[1], 16)
            sp.wait_ge(stream_dma[0], 16 * (UNITS // 2 + B))
            sp.wait_ge(stream_dma[1], 16 * (UNITS // 2 + B - 1 + TT))

        @block.gpsimd
        def _(pool):
            nc.gpsimd.memset(ones[:], 1.0).then_inc(pool_step, 1)
            nc.gpsimd.memset(base[:, 6, 2, 0:2 * P], 0.0).then_inc(pool_step, 1)
            nc.gpsimd.memset(onesr[:].bitcast(F32), 1.0).then_inc(pool_step, 1)
            nc.gpsimd.memset(sel3[:], 0.0).then_inc(pool_step, 1)
            nc.gpsimd.memset(eye4[:], 0.0).then_inc(pool_step, 1)
            pool.wait_ge(pool_step, 5)
            nc.gpsimd.affine_select(out=ident[:], in_=ones[:], compare_op=ALU.is_equal, fill=0.0, base=0,
                                    pattern=[[-1, P]], channel_multiplier=1).then_inc(consts_ready, 1)
            nc.gpsimd.affine_select(out=sel3[:], in_=sel3[:], compare_op=ALU.not_equal, fill=1.0, base=0,
                                    pattern=[[-4, 32], [-1, 4]], channel_multiplier=1).then_inc(consts_ready, 1)
            nc.gpsimd.affine_select(out=eye4[:], in_=eye4[:], compare_op=ALU.not_equal, fill=1.0, base=0,
                                    pattern=[[-1, 4], [1, 4]], channel_multiplier=0).then_inc(consts_ready, 1)
            nc.gpsimd.affine_select(out=sel2[:], in_=ones[0:16, :], compare_op=ALU.is_ge, fill=0.0, base=0,
                                    pattern=[[1, P]], channel_multiplier=-8).then_inc(pool_step, 1)
            pool.wait_ge(pool_step, 6)
            nc.gpsimd.affine_select(out=sel2[:], in_=sel2[:], compare_op=ALU.is_ge, fill=0.0, base=7,
                                    pattern=[[-1, P]], channel_multiplier=8).then_inc(consts_ready, 1)
            pool.wait_ge(consts_ready, 4)

            for kc in range(KC):
                pool.wait_ge(w1_loaded[kc], 16)
                nc.gpsimd.tensor_tensor(w1sq[:, kc], w1s[:, kc], w1s[:, kc], ALU.mult).then_inc(w1sq_ready, 1)
            nc.gpsimd.tensor_tensor(two_eye[:], ident[:], ident[:], ALU.add).then_inc(pool_step, 1)
            for kc in range(KC):
                pool.wait_ge(w0_hi, kc + 1)
                nc.gpsimd.tensor_tensor(w0s[:, 1, kc], w0raw[:, kc], w0s[:, 0, kc].bitcast(F32),
                                        ALU.subtract).then_inc(w0_lo, 1)
            for c in range(2):
                for g in range(2):
                    for q in range(2):
                        src = ident[:, q * 64:(q + 1) * 64].rearrange("p (r b) -> p r b", b=B)[:, :, 4 * g:4 * g + 4]
                        dst = perm[:, 2 * c + g].rearrange("p (u v r b) -> p u v r b", u=2, v=2, b=4)
                        for i in range(2):
                            at = dst[:, q, i] if c else dst[:, i, q]
                            nc.gpsimd.tensor_copy(at, src).then_inc(perm_ready, 1)
            pool.wait_ge(mask_ready, 2)
            pool.wait_ge(squared, 2)
            for b in range(2):
                nc.gpsimd.tensor_scalar(amk[:, b], asq[:, 0].bitcast(F32), mask[:, 0, b:b + 1], None,
                                        ALU.mult).then_inc(amk_ready, 1)
            pool.wait_ge(d_first_loaded, 16)
            pool.wait_ge(w0nat_loaded, 16)
            for cc in range(KC):
                row = base[:, 0, cc, :]
                pool.wait_ge(bank_free, BANKS + cc + 1)
                nc.gpsimd.tensor_tensor(row, row, d_first, ALU.mult).then_inc(fix_step, 1)
                pool.wait_ge(fix_step, 2 * cc + 1)
                nc.gpsimd.tensor_tensor(row, row, w0nat[:, cc], ALU.add).then_inc(fix_step, 1)
                pool.wait_ge(fix_step, 2 * cc + 2)
                blk = base[:, 0, cc, cc * P:(cc + 1) * P]
                nc.gpsimd.tensor_tensor(blk, blk, two_eye[:], ALU.add).then_inc(fixed, 1)
            with pool.Fori(1, B // 2) as pair:
                for j in range(2):
                    pool.wait_ge(ac_done, pair * 8 + (4 * j - 4))
                    keep = mask[:].rearrange("p g b -> p (g b)")[:, bass.ds(pair * 2 + j, 1)]
                    nc.gpsimd.tensor_tensor(amk[:, j], asq[:, bass.ds(pair // 2, 1), :].rearrange("p o n -> p (o n)")
                                            .bitcast(F32), keep.to_broadcast([P, D]),
                                            ALU.mult).then_inc(amk_ready, 1)

        @block.scalar
        def _(act):
            act.wait_ge(pool_step, 1)
            nc.scalar.activation(lns[:, 15, 0:1], ones[:, 0:1], ACT.Sqrt)

            def w0_high(kc):
                act.wait_ge(w0_eyed, kc + 1)
                nc.scalar.copy(w0s[:, 0, kc], w0raw[:, kc]).then_inc(w0_hi, 1)

            act.wait_ge(ys_ready, 1)

            def first_high(kc):
                act.wait_ge(w0_eyed, kc + 1)
                nc.scalar.activation(m0s[:, 0, kc], w0raw[:, kc], ACT.Copy, scale=ys[:, 0, kc:kc + 1]
                                     ).then_inc(m0_hi, 1)
                act.wait_ge(w1_loaded[kc], 16)
                nc.scalar.copy(w1r[:, 0, kc], w1s[:, kc]).then_inc(w1_hi, 1)

            for kc in range(3):
                first_high(kc)
                if kc == 0:
                    act.wait_ge(ln_step, 6)
                    nc.scalar.activation(lns[:, 12, 0:B], lns[:, 2, 0:B], ACT.Sqrt).then_inc(ln_root, 1)
            act.wait_ge(d2_done, 1)
            nc.scalar.copy(d2_rows, aux[1][:, 0:P]).then_inc(d2_copied, 1)
            w0_high(0)
            act.wait_ge(d_step, 1)
            nc.scalar.activation(lns[:, 4], lns[:, 3], ACT.Sqrt).then_inc(d_root, 1)
            first_high(3)
            nc.scalar.activation(lns[:, 15, 0:1], ones[:, 0:1], ACT.Gelu)
            w0_high(1)
            act.wait_ge(h_done, 1)
            nc.scalar.copy(h_rows, aux[1][:, P:2 * P]).then_inc(h_copied, 1)
            w0_high(2)
            w0_high(3)
            act.wait_ge(d_turned, 1)
            nc.scalar.copy(d_rows, aux[1][0:B * KC, 2 * P:3 * P]).then_inc(d_copied, 1)

            def r_high(b, kc):
                act.wait_ge(r_eyed, b * KC + (kc + 1 - KC))
                nc.scalar.copy(rs[:, kc, 0], rtmp[:, kc % RTMP]).then_inc(r_hi, 1)

            def evacuate_base(b, chunks=range(KC)):
                for cc in chunks:
                    act.wait_ge(tile_done, b * KC + (cc + 1))
                    nc.scalar.copy(base[:, b, cc, :], tiles[cc][:]).then_inc(bank_free, 1)

            act.wait_ge(z_ready, 1)
            nc.scalar.activation(lns[:, 15], lns[:, 11], ACT.Gelu).then_inc(h_ready, 1)
            r_high(1, 0)
            evacuate_base(0, (0, 1))
            r_high(1, 1)
            evacuate_base(0, (2, 3))
            r_high(1, 2)
            r_high(1, 3)

            def base_step(b):
                for kc in range(KC - 1):
                    r_high(b + 1, kc)
                evacuate_base(b)
                r_high(b + 1, KC - 1)

            with act.Fori(1, LOOPED + 1) as b:
                base_step(b)
            act.wait_ge(ab_ready, 1)
            act.wait_ge(perm_ready, 16)
            nc.scalar.copy(asp[0:64, :], ab[64:128, :]).then_inc(a_hi, 1)
            nc.scalar.copy(asp[64:128, :], ab[64:128, :]).then_inc(a_hi, 1)

            def x_high(b, h, cp, next_half=0):
                act.wait_ge(x_loaded[cp], b * 32 + 16 * (h + 1))
                if next_half:
                    act.wait_ge(tile_done, b * 8 + (4 * B + 4 * h - 4))
                nc.scalar.copy(xs[:, h, 0, 2 * cp:2 * cp + 2, :], xr[:, cp]).then_inc(x_hi, 1)

            def squared_rows(to, g, bank, n):
                act.wait_ge(perm_done, n)
                nc.scalar.copy(to[:, g], bank[:]).then_inc(squared, 1)

            x_high(0, 0, 0)
            x_high(0, 0, 1)
            r_high(6, 0)
            r_high(6, 1)
            act.wait_ge(c_done, 1)
            nc.scalar.copy(c_part, aux[1][64:128, :]).then_inc(c_halved, 1)
            squared_rows(asq, 0, acc2, 1)
            squared_rows(asq, 1, aux[0], 2)
            act.wait_ge(c_step, 3)
            nc.scalar.copy(csp[0:64, :], ct).then_inc(c_hi, 1)
            nc.scalar.copy(csp[64:128, :], ct).then_inc(c_hi, 1)
            evacuate_base(5, (0, 1))
            r_high(6, 2)
            evacuate_base(5, (2, 3))
            r_high(6, 3)

            def p_high(b, parity, cc):
                act.wait_ge(p_summed, b * KC + (cc + 1))
                nc.scalar.copy(p_split(parity)[:, 0, cc], base[:, b, cc, :]).then_inc(p_hi, 1)

            squared_rows(csq, 0, acc2, 3)
            squared_rows(csq, 1, aux[0], 4)
            r_high(7, 0)
            r_high(7, 1)
            evacuate_base(6, (0, 1))
            r_high(7, 2)
            evacuate_base(6, (2, 3))
            r_high(7, KC - 1)
            for cc in range(KC):
                p_high(0, 0, cc)
            evacuate_base(B - 1)

            def evacuate_out(b, h, tt):
                act.wait_ge(tile_done, b * 8 + (4 * B + 4 * h + tt + 1))
                if tt == 0:
                    act.wait_ge(stream_dma[h], b * 16 + 16 * (UNITS // 2))
                nc.scalar.copy(stream[:, h, tt, :], tiles[tt][:]).then_inc(bank_free, 1)

            def main_step(b, parity, last=False):
                for cp in range(2):
                    x_high(b, 1, cp, 1)
                    evacuate_out(b, 0, cp)
                for tt in (2, 3):
                    evacuate_out(b, 0, tt)
                for cp in range(2):
                    if not last:
                        x_high(b + 1, 0, cp, 1)
                        p_high(b + 1, 1 - parity, 2 * cp)
                        p_high(b + 1, 1 - parity, 2 * cp + 1)
                    evacuate_out(b, 1, cp)
                for tt in (2, 3):
                    evacuate_out(b, 1, tt)

            with act.Fori(0, B // 2 - 1) as pair:
                main_step(pair * 2, 0)
                main_step(pair * 2 + 1, 1)
            main_step(B - 2, 0)
            main_step(B - 1, 1, last=True)

        @block.vector
        def _(dve):
            small = [0]

            def step(instruction):
                small[0] += 1
                instruction.then_inc(ln_step, 1)
                dve.wait_ge(ln_step, small[0])

            def row(i, n=KC * B):
                return lns[:, i, 0:n]

            def by_chunk(i):
                return lns[:, i].rearrange("p (k b) -> p k b", k=KC)

            def turned(i):
                return aux[0][:, i * P:(i + 1) * P].rearrange("p (k c) -> p k c", k=KC)[:, :, 0:B]

            def over_chunks(i):
                return lns[:, i, 0:B].rearrange("p (k b) -> p k b", k=1).to_broadcast([P, KC, B])

            def over_partitions(i):
                return row(i, B).rearrange("p (b o) -> p b o", o=1)

            dve.wait_ge(cond_loaded, 16)
            step(nc.vector.tensor_reduce(over_partitions(14), cond[:].rearrange("p k b -> p b k"),
                                         mybir.AxisListType.X, ALU.add))
            nc.vector.tensor_scalar(ys[:].rearrange("p b k -> p k b"), cond[:], YS_SCALE, None,
                                    ALU.mult).then_inc(ys_ready, 1)
            dve.wait_ge(ys_ready, 1)
            dve.wait_ge(pool_step, 2)
            nc.vector.tensor_tensor(ysq[:, :, 0:B], ys[:].rearrange("p b k -> p k b"),
                                    ys[:].rearrange("p b k -> p k b"), ALU.mult).then_inc(ysq_ready, 1)

            def add_two(kc):
                dve.wait_ge(w0_loaded[kc], 16)
                blk = w0raw[:, kc, kc * P:(kc + 1) * P]
                nc.vector.scalar_tensor_tensor(blk, ident[:], 2.0, blk, ALU.mult, ALU.add).then_inc(w0_eyed, 1)

            def first_low(kc):
                dve.wait_ge(m0_hi, kc + 1)
                nc.vector.scalar_tensor_tensor(m0s[:, 1, kc], w0raw[:, kc], ys[:, 0, kc:kc + 1],
                                               m0s[:, 0, kc].bitcast(F32), ALU.mult, ALU.subtract).then_inc(m0_lo, 1)
                dve.wait_ge(w1_hi, kc + 1)
                nc.vector.tensor_tensor(w1r[:, 1, kc], w1s[:, kc], w1r[:, 0, kc].bitcast(F32),
                                        ALU.subtract).then_inc(w1_lo, 1)

            dve.wait_ge(consts_ready, 1)
            add_two(0)
            dve.wait_ge(sum_done, 1)
            step(nc.vector.tensor_scalar(row(0, B), aux[0][:, 0:B], 1.0 / D, None, ALU.mult))
            step(nc.vector.tensor_tensor(by_chunk(1), cond[:], over_chunks(0), ALU.subtract))
            step(nc.vector.tensor_tensor(row(5), row(1), row(1), ALU.mult))
            step(nc.vector.tensor_reduce(over_partitions(13), row(5).rearrange("p (k b) -> p b k", k=KC),
                                         mybir.AxisListType.X, ALU.add))

            first_low(0)
            add_two(1)
            dve.wait_ge(sum_done, 2)
            step(nc.vector.tensor_scalar(row(2, B), aux[0][:, 64:64 + B], 1.0 / D, LN_EPS, ALU.mult, ALU.add))
            first_low(1)
            add_two(2)
            dve.wait_ge(ln_root, 1)
            step(nc.vector.reciprocal(row(5, B), row(12, B)))
            step(nc.vector.scalar_tensor_tensor(row(6, B), row(5, B), -0.5, row(2, B), ALU.mult, ALU.mult))
            step(nc.vector.tensor_tensor(row(7, B), row(6, B), row(5, B), ALU.mult))
            step(nc.vector.scalar_tensor_tensor(row(0, B), row(7, B), 1.5, row(5, B), ALU.add, ALU.mult))
            first_low(2)
            add_two(3)
            dve.wait_ge(prm_loaded, 48)
            step(nc.vector.tensor_tensor(by_chunk(8), by_chunk(1), over_chunks(0), ALU.mult))
            step(nc.vector.tensor_tensor(by_chunk(9), by_chunk(8), prm[:, 1].to_broadcast([P, KC, B]), ALU.mult))
            nc.vector.tensor_tensor(ae[:, :, 0:B], by_chunk(9), prm[:, 2].to_broadcast([P, KC, B]),
                                    ALU.add).then_inc(ae_ready, 1)
            dve.wait_ge(d2_turned, 1)
            nc.vector.tensor_scalar(by_chunk(3), turned(1), D_EPS, None, ALU.add).then_inc(d_step, 1)
            dve.wait_ge(d_root, 1)
            nc.vector.reciprocal(row(6), row(4)).then_inc(d_step, 1)
            dve.wait_ge(d_step, 2)
            nc.vector.scalar_tensor_tensor(row(7), row(6), -0.5, row(3), ALU.mult, ALU.mult).then_inc(d_step, 1)
            dve.wait_ge(d_step, 3)
            nc.vector.tensor_tensor(row(8), row(7), row(6), ALU.mult).then_inc(d_step, 1)
            dve.wait_ge(d_step, 4)
            nc.vector.scalar_tensor_tensor(dts[:, 0].rearrange("p b k -> p k b"), by_chunk(8), 1.5, by_chunk(6),
                                           ALU.add, ALU.mult).then_inc(d_step, 1)
            dve.wait_ge(d_step, 5)
            nc.vector.tensor_copy(dth[:], dts[:, 0]).then_inc(d_root, 1)
            dve.wait_ge(d_root, 2)
            nc.vector.tensor_tensor(dts[:, 1], dts[:, 0], dth[:].bitcast(F32), ALU.subtract).then_inc(d_step, 1)
            dve.wait_ge(d_step, 6)

            for u in range(2):
                col = dts[:, u, 1].rearrange("p (k m) -> p k m", m=1).to_broadcast([P, KC, P])
                nc.vector.tensor_tensor(dgn[:, u], eye_wide, col, ALU.mult).then_inc(dgn_ready, 1)
            first_low(3)
            dve.wait_ge(consts_ready, 4)
            nc.vector.tensor_reduce(mask[:, 0], sel3[:].rearrange("p q b -> p b q"), mybir.AxisListType.X,
                                    ALU.add).then_inc(mask_ready, 1)
            dve.wait_ge(mask_ready, 1)
            nc.vector.tensor_copy(mask[:, 1], mask[:, 0]).then_inc(mask_ready, 1)

            def r_scale(b, kc, first):
                slot = rtmp[:, kc % RTMP]
                if not first and kc == KC - 1:
                    dve.wait_ge(tile_done, b * KC)
                elif not first:
                    dve.wait_ge(r_used, b * (KC - 1) + (kc + 1 - 2 * (KC - 1)))
                if not first or kc >= RTMP:
                    dve.wait_ge(r_lo, b * KC + (kc + 1 - RTMP - KC))
                d = dbc if first else dbs
                nc.vector.scalar_tensor_tensor(slot, w1s[:, kc], ys[:, bass.ds(b, 1), kc], d[:], ALU.mult,
                                               ALU.mult).then_inc(r_scaled, 1)
                dve.wait_ge(r_scaled, b * KC + (kc + 1 - KC))
                blk = slot[:, kc * P:(kc + 1) * P]
                nc.vector.tensor_tensor(blk, blk, ident[:], ALU.add).then_inc(r_eyed, 1)

            def r_low(b, kc):
                dve.wait_ge(r_hi, b * KC + (kc + 1 - KC))
                nc.vector.tensor_tensor(rs[:, kc, 1], rtmp[:, kc % RTMP], rs[:, kc, 0].bitcast(F32),
                                        ALU.subtract).then_inc(r_lo, 1)

            def x_low(b, h, cp):
                unit = b * 4 + (2 * h + cp + 1)
                dve.wait_ge(x_hi, unit)
                nc.vector.tensor_tensor(xs[:, h, 1, 2 * cp:2 * cp + 2, :], xr[:, cp],
                                        xs[:, h, 0, 2 * cp:2 * cp + 2, :].bitcast(F32),
                                        ALU.subtract).then_inc(x_lo, 1)

            def h_columns(b):
                dve.wait_ge(acc2_steps, b * 4 - 3)
                nc.vector.tensor_tensor(hz, lns[:, 15].rearrange("p (k o b) -> p k o b", k=KC, o=1)
                                        .to_broadcast([P, KC, 4, B]),
                                        eye4[:, bass.ds(b - 1, 1), :].rearrange("p o (r c) -> p o r c", c=1)
                                        .to_broadcast([P, KC, 4, B]), ALU.mult).then_inc(hz_ready, 1)

            def r_build(b, columns=False):
                dve.wait_ge(dbs_loaded, b * 16 - 16)
                r_scale(b, 0, False)
                r_scale(b, 1, False)
                r_low(b, 0)
                r_low(b, 1)
                r_scale(b, 2, False)
                r_low(b, 2)
                r_scale(b, 3, False)
                if columns:
                    h_columns(b)
                r_low(b, 3)

            dve.wait_ge(h_turned, 1)
            nc.vector.tensor_tensor(by_chunk(11), turned(2), prm[:, 0].to_broadcast([P, KC, B]),
                                    ALU.add).then_inc(z_ready, 1)
            dve.wait_ge(dbc_ready, 1)
            r_scale(1, 0, True)
            r_scale(1, 1, True)
            r_low(1, 0)
            dve.wait_ge(h_ready, 1)
            h_columns(1)
            r_scale(1, 2, True)
            r_low(1, 1)
            r_scale(1, 3, True)
            r_low(1, 2)
            r_low(1, 3)
            with dve.Fori(2, LOOPED + 1) as b:
                r_build(b, columns=True)
            r_build(LOOPED + 1)
            dve.wait_ge(acc2_steps, UNITS + 1)
            nc.vector.tensor_copy(ab, acc2[:]).then_inc(ab_ready, 1)
            dve.wait_ge(a_hi, 2)
            nc.vector.tensor_tensor(asp[64:128, :], ab[64:128, :], asp[64:128, :].bitcast(F32),
                                    ALU.subtract).then_inc(a_lo, 1)
            dve.wait_ge(bt_done, 1)
            nc.vector.tensor_tensor(ysb[:].rearrange("p k (r b) -> p k r b", b=B),
                                    aux[0][:, 0:KC * 64].rearrange("p (k r b) -> p k r b", k=KC, b=B),
                                    ys[:].rearrange("p b (k o) -> p k o b", o=1).to_broadcast([P, KC, RANK, B]),
                                    ALU.mult).then_inc(ysb_ready, 1)
            dve.wait_ge(dbs_loaded, 16 * 5)
            r_scale(6, 0, False)
            r_scale(6, 1, False)
            r_low(6, 0)
            r_low(6, 1)
            dve.wait_ge(c_halved, 1)
            dve.wait_ge(d64_loaded, 16 * RANK)
            nc.vector.tensor_tensor(ct, aux[1][0:64, :], c_part, ALU.add).then_inc(c_step, 1)
            dve.wait_ge(c_step, 1)
            nc.vector.tensor_tensor(ct, ct, d64, ALU.mult).then_inc(c_step, 1)
            dve.wait_ge(c_step, 2)
            nc.vector.tensor_tensor(ct, ct, ab[0:64, :], ALU.add).then_inc(c_step, 1)
            r_scale(6, 2, False)
            dve.wait_ge(c_hi, 2)
            nc.vector.tensor_tensor(csp[64:128, :], ct, csp[0:64, :].bitcast(F32), ALU.subtract).then_inc(c_lo, 1)
            r_low(6, 2)
            x_low(0, 0, 0)
            r_scale(6, 3, False)
            r_low(6, 3)
            x_low(0, 0, 1)
            r_build(7)

            def p_sum(b, cc):
                dve.wait_ge(ac_done, b * KC + (cc + 1))
                dve.wait_ge(bank_free, b * KC + (BANKS + cc + 1))
                nc.vector.tensor_tensor(base[:, b, cc, :], aux[cc % 2][:], base[:, b, cc, :],
                                        ALU.add).then_inc(p_summed, 1)

            def p_low(b, parity, cc):
                dve.wait_ge(p_hi, b * KC + (cc + 1))
                nc.vector.tensor_tensor(p_split(parity)[:, 1, cc], base[:, b, cc, :],
                                        p_split(parity)[:, 0, cc].bitcast(F32), ALU.subtract).then_inc(p_lo, 1)

            dve.wait_ge(fixed, KC)
            for cc in range(KC):
                p_sum(0, cc)
            for cc in range(KC):
                p_low(0, 0, cc)

            def main_step(b, parity, last=False):
                for cp in range(2):
                    x_low(b, 1, cp)
                if last:
                    return
                for cc in range(KC):
                    p_sum(b + 1, cc)
                for cp in range(2):
                    x_low(b + 1, 0, cp)
                    p_low(b + 1, 1 - parity, 2 * cp)
                    p_low(b + 1, 1 - parity, 2 * cp + 1)

            with dve.Fori(0, B // 2 - 1) as pair:
                main_step(pair * 2, 0)
                main_step(pair * 2 + 1, 1)
            main_step(B - 2, 0)
            main_step(B - 1, 1, last=True)

        @block.tensor
        def _(pe):
            pe.sem_inc(bank_free, BANKS)
            pe.wait_ge(pool_step, 1)

            def warm_up(n):
                for _ in range(n):
                    nc.tensor.matmul(tiles[BANKS - 1][:, 0:P], ones[:], ones[:], start=True, stop=True)

            warm_up(WARM_UP[0])
            pe.wait_ge(ln_step, 1)
            nc.tensor.matmul(aux[0][:, 0:B], ones[:], lns[:, 14, 0:B], start=True, stop=True).then_inc(sum_done, 1)
            warm_up(WARM_UP[1])
            pe.wait_ge(ln_step, 5)
            nc.tensor.matmul(aux[0][:, 64:64 + B], ones[:], lns[:, 13, 0:B], start=True,
                             stop=True).then_inc(sum_done, 1)
            warm_up(WARM_UP[2])

            def narrow(at, small, wide, ready=None):
                for kc in range(KC):
                    if ready:
                        pe.wait_ge(ready, kc + 1)
                    for g in range(KC):
                        last = nc.tensor.matmul(aux[1][32 * g:32 * g + 32, at * P:(at + 1) * P], small[:, kc],
                                                wide[:, kc, g * P:(g + 1) * P], start=kc == 0, stop=kc == KC - 1,
                                                skip_group_check=True)
                return last

            def first_tiles(kc, chunks=range(KC)):
                pe.wait_ge(m0_lo, kc + 1)
                passes = (((0, 0), (1, 0)), ((0, 1),)) if kc == 0 else (((0, 0), (0, 1), (1, 0)),)
                for group in passes:
                    pe.wait_ge(w1_hi if kc == 0 and group is passes[0] else w1_lo, kc + 1)
                    for cc in chunks:
                        for u, v in group:
                            last = nc.tensor.matmul(tiles[cc][:], m0s[:, u, kc, cc * P:(cc + 1) * P], w1r[:, v, kc],
                                                    start=kc == 0 and (u, v) == (0, 0),
                                                    stop=kc == KC - 1 and (u, v) == (1, 0))
                        if kc == KC - 1:
                            last.then_inc(tile_done, 1)

            first_tiles(0)
            pe.wait_ge(ysq_ready, 1)
            narrow(0, ysq, w1sq, ready=w1sq_ready).then_inc(d2_done, 1)
            first_tiles(1, (0, 1))
            pe.wait_ge(d2_copied, 1)
            nc.tensor.transpose(aux[0][:, P:2 * P], d2_rows, ident[:]).then_inc(d2_turned, 1)
            first_tiles(1, (2, 3))
            pe.wait_ge(wm_loaded, 16)
            pe.wait_ge(ae_ready, 1)
            narrow(1, ae, wms).then_inc(h_done, 1)
            first_tiles(2, (0, 1))
            pe.wait_ge(h_copied, 1)
            nc.tensor.transpose(aux[0][:, 2 * P:3 * P], h_rows, ident[:]).then_inc(h_turned, 1)
            first_tiles(2, (2, 3))
            pe.wait_ge(dgn_ready, 2)
            for u in range(2):
                last = nc.tensor.matmul(dbc[:], onesr[:], dgn[:, u].rearrange("p k m -> p (k m)"), start=u == 0,
                                        stop=u == 1)
            last.then_inc(dbc_ready, 1)
            nc.tensor.transpose(aux[1][0:B * KC, 2 * P:3 * P], dts[:, 0].rearrange("p b k -> p (b k)"),
                                ident[:]).then_inc(d_turned, 1)
            pe.wait_ge(b2_loaded, 16)
            pe.wait_ge(consts_ready, 4)
            nc.tensor.matmul(acc2[:], sel2[:], b2s, start=True, stop=True,
                             skip_group_check=True).then_inc(acc2_steps, 1)
            first_tiles(3)

            def w2_unit(b, j):
                pe.wait_ge(hz_ready, b)
                pe.wait_ge(stream_dma[j % 2], b * 32 + 16 * (j // 2 - 1))
                for g in range(4):
                    last = nc.tensor.matmul(acc2[32 * g:32 * g + 32, :], hz[:, j], stream[:, j % 2, g, :],
                                            start=False, stop=True, skip_group_check=True)
                last.then_inc(acc2_steps, 1)

            def base_tiles(b, units=False, between=None):
                for kc in range(KC):
                    pe.wait_ge(w0_lo, kc + 1)
                    passes = (((0, 0), (1, 0)), ((0, 1),)) if kc == 0 else (((0, 0), (0, 1), (1, 0)),)
                    for group in passes:
                        if group[0][1] == 0 and kc == 0:
                            pe.wait_ge(r_hi, b * KC + (1 - KC))
                        else:
                            pe.wait_ge(r_lo, b * KC + (kc + 1 - KC))
                        for cc in range(KC):
                            if kc == 0 and group is passes[0]:
                                pe.wait_ge(bank_free, b * KC + (cc + 1))
                            cols = slice(cc * P, (cc + 1) * P)
                            for u, v in group:
                                last = nc.tensor.matmul(tiles[cc][:], w0s[:, u, kc, cols], rs[:, kc, v],
                                                        start=kc == 0 and (u, v) == (0, 0),
                                                        stop=kc == KC - 1 and (u, v) == (1, 0))
                            if kc == KC - 1:
                                last.then_inc(tile_done, 1)
                            elif cc == KC - 1 and group is passes[-1]:
                                last.then_inc(r_used, 1)
                    if units:
                        w2_unit(b, kc)
                    if between:
                        between(b, kc)

            def rank_tile(b, parity, cc, group, first=False):
                pe.wait_ge(amk_ready, b + 1)
                if not first or cc >= 2:
                    pe.wait_ge(p_summed, b * KC + (cc - 1))
                rows = csq[:, bass.ds(group, 1), :].rearrange("p o n -> p (o n)")
                nc.tensor.matmul(aux[cc % 2][:], amk[:, parity, cc * P:(cc + 1) * P], rows, start=True,
                                 stop=True).then_inc(ac_done, 1)

            def permute(bank, which, rows):
                nc.tensor.matmul(bank[:], perm[:, which], rows, start=True, stop=True).then_inc(perm_done, 1)

            with pe.Fori(1, LOOPED + 1) as b:
                base_tiles(b, units=True)

            def columns_and_c(b, kc):
                if kc == 0:
                    pe.wait_ge(ab_ready, 1)
                    for c in range(KC):
                        last = nc.tensor.transpose(aux[0][:, c * 64:(c + 1) * 64], ab[0:64, c * P:(c + 1) * P],
                                                   ident[0:64, 0:64])
                    last.then_inc(bt_done, 1)
                elif kc == 1:
                    pe.wait_ge(ysb_ready, 1)
                    for i in range(2):
                        for g in range(2):
                            c = 2 * g + i
                            last = nc.tensor.matmul(aux[1][64 * g:64 * g + 64, :], ysb[:, c], w1s[:, c], start=i == 0,
                                                    stop=i == 1, skip_group_check=True)
                    last.then_inc(c_done, 1)
                    pe.wait_ge(a_lo, 1)
                    permute(acc2, 0, asp)
                    permute(aux[0], 1, asp)

            base_tiles(5, between=columns_and_c)

            def permute_c(b, kc):
                if kc != 0:
                    return
                pe.wait_ge(c_lo, 1)
                pe.wait_ge(squared, 2)
                permute(acc2, 2, csp)
                permute(aux[0], 3, csp)

            base_tiles(6, between=permute_c)
            pe.wait_ge(squared, 4)

            def first_rank_tiles(b, kc):
                for cc in ((0, 1), (2, 3), (), ())[kc]:
                    rank_tile(0, 0, cc, 0, first=True)

            base_tiles(7, between=first_rank_tiles)

            def main_step(b, parity, group, last=False):
                pe.wait_ge(p_lo, b * KC + KC)
                for h in range(HALVES):
                    pe.wait_ge(x_lo, b * 4 + (2 * h + 2))
                    for tt in range(TT):
                        pe.wait_ge(bank_free, b * 8 + (4 * B + 4 * h + tt + 1))
                        toks = slice(tt * P, (tt + 1) * P)
                        n = 0
                        for cc in range(KC):
                            for u, v in ((0, 0), (0, 1), (1, 0)):
                                mm = nc.tensor.matmul(tiles[tt][:], xs[:, h, u, cc, toks],
                                                      p_split(parity)[:, v, cc], start=n == 0, stop=n == 11)
                                n += 1
                        mm.then_inc(tile_done, 1)
                        if h == 0 and not last:
                            rank_tile(b + 1, 1 - parity, tt, group)

            with pe.Fori(0, B // 2 - 1) as pair:
                main_step(pair * 2, 0, pair // 2)
                main_step(pair * 2 + 1, 1, (pair + 1) // 2)
            main_step(B - 2, 0, 1)
            main_step(B - 1, 1, None, last=True)


def kernel(**inputs):
    import numpy as np
    import concourse.bacc as bacc
    from concourse.bass_utils import run_bass_kernel_spmd

    def chunked(a):
        return np.ascontiguousarray(a.reshape(KC, P, -1).transpose(1, 0, 2))

    def columns(a):
        return np.ascontiguousarray(a.reshape(KC, P).T)

    a = {k: np.asarray(v) for k, v in inputs.items()}
    x = a["x"].reshape(B, HALVES, P, TT, 2, 2, P)
    x = np.ascontiguousarray(x.transpose(0, 1, 4, 6, 5, 3, 2)).reshape(B, HALVES, 2, P, 2, TH)
    w2 = a["L0_cond_w2"].reshape(KC, P, 2, D, 2, 4)[:, :, ::-1]
    w2 = np.ascontiguousarray(w2.transpose(5, 0, 1, 2, 4, 3)).reshape(UNITS, P, 4, D)
    b2 = np.ascontiguousarray(a["L0_cond_b2"].reshape(2, D, RANK)[::-1].transpose(0, 2, 1)).reshape(16, D)
    arrays = {
        "xT": x,
        "condT": chunked(a["cond_1024"].T),
        "w0T": chunked(a["L0_cond_base_layer"].T),
        "w0n": chunked(a["L0_cond_base_layer"]),
        "w1n": chunked(a["L1_cond_weight"]),
        "wm": chunked(a["L0_cond_w1"]),
        "b1c": columns(a["L0_cond_b1"]),
        "lngc": columns(a["L0_cond_ln_g"]),
        "lnbc": columns(a["L0_cond_ln_b"]),
        "w2u": w2,
        "b2q": b2,
    }
    nc = bacc.Bacc("TRN2", target_bir_lowering=False, num_devices=1)
    aps = {k: nc.dram_tensor(f"in_{k}", v.shape, F32, kind="ExternalInput").ap() for k, v in arrays.items()}
    out = nc.dram_tensor("out", (B, HALVES, P, TT, D), F32, kind="ExternalOutput").ap()
    cond_residual_kernel(nc, out=out, **aps)
    r = run_bass_kernel_spmd(nc, [{f"in_{k}": v for k, v in arrays.items()}], core_ids=[0])
    return r.results[0]["out"].reshape(B, T, D)
```
